# Optimizing a Trainium2 kernel written in Bass

```python
import numpy as np
import jax
import jax.numpy as jnp

def _softmax(x, axis=-1):
    return jax.nn.softmax(x, axis=axis)

def _gelu(x):
    return jax.nn.gelu(x, approximate=True)

def _silu(x):
    return jax.nn.silu(x)

def _sigmoid(x):
    return jax.nn.sigmoid(x)

def _layernorm(x, axis=-1, eps=1e-05):
    m = jnp.mean(x, axis=axis, keepdims=True)
    v = jnp.var(x, axis=axis, keepdims=True)
    return (x - m) / jnp.sqrt(v + eps)

def _scatter_add(tgt, idx, src, axis=0):
    return tgt.at[idx].add(src)

def _segment_sum(src, seg, n):
    return jax.ops.segment_sum(src, seg, n)
kernel_name = 'mk_xattn_ffn_d1_seqx_r8_84845f'

def setup_inputs(seed: int=0):
    np.random.seed(seed)
    _w = jnp.asarray

    def _rec_inputs():
        import jax
        import jax.numpy as jnp
        _rk = jax.random.key(seed)
        x = 0.5 + 0.2887 * jax.random.normal(jax.random.fold_in(_rk, 1), (4, 256, 256), jnp.float32)
        _lenS = 256 - jax.random.randint(jax.random.fold_in(_rk, 7), (4,), 0, max(1, 256 // 4) + 1, jnp.int32)
        _lenS2 = 256 - jax.random.randint(jax.random.fold_in(_rk, 8), (4,), 0, max(1, 256 // 4) + 1, jnp.int32)
        _ctx_512P = jax.random.normal(jax.random.fold_in(_rk, 11), (4, 16, 64), jnp.float32)
        _ctx_512c = jax.random.dirichlet(jax.random.fold_in(_rk, 511), 0.3 * jnp.ones((16,), jnp.float32), (4, 256))
        _ctx_512t = jnp.einsum('bsk,bkd->bsd', _ctx_512c, _ctx_512P)
        _ctx_512t = _ctx_512t * jax.lax.rsqrt(jnp.mean(jnp.square(_ctx_512t)) + 1e-12) * 0.953939
        ctx_512 = -0.000392918 + 0.999932 * (_ctx_512t + 0.3 * jax.random.normal(jax.random.fold_in(_rk, 611), (4, 256, 64), jnp.float32))
        return (x, ctx_512)
    x, ctx_512 = _rec_inputs()

    def _L0_xattn_setup():
        import jax, jax.numpy as jnp
        import numpy as np
        B, N, D = (16, 256, 64)
        H = 4
        TOP_K_RATIO = 0.3
        key = jax.random.key(seed)
        k1, k2, k3, k4 = jax.random.split(key, 4)
        h = jax.random.normal(k1, (B, N, D), dtype=jnp.float32)
        adj_raw = jax.random.uniform(k2, (B, N, N), dtype=jnp.float32)
        lim = 1.0 / np.sqrt(D)
        Wq = jax.random.uniform(k3, (D, D), minval=-lim, maxval=lim, dtype=jnp.float32)
        Wk = jax.random.uniform(k4, (D, D), minval=-lim, maxval=lim, dtype=jnp.float32)
        gamma_raw = jnp.float32(-0.85)
        return {'h': h, 'adj_raw': adj_raw, 'Wq': Wq, 'Wk': Wk, 'gamma_raw': gamma_raw}
    _L0_xattn_all = _L0_xattn_setup()
    _L0_xattn_in = {k: v for k, v in _L0_xattn_all.items() if k in ('Wq', 'Wk', 'gamma_raw')}
    del _L0_xattn_all

    def _L0_ffn_setup():
        import jax, jax.numpy as jnp
        import numpy as np
        B, S, D, FF, E = (4, 256, 256, 1024, 2)
        key = jax.random.key(seed)
        k0, k1, k2, k3, k4 = jax.random.split(key, 5)
        s = 0.02
        return {'hidden_states': jax.random.normal(k0, (B, S, D), jnp.float32), 'gate_w': jax.random.normal(k1, (E, D), jnp.float32) * s, 'w_gate': jax.random.normal(k2, (E, FF, D), jnp.float32) * s, 'w_up': jax.random.normal(k3, (E, FF, D), jnp.float32) * s, 'w_down': jax.random.normal(k4, (E, D, FF), jnp.float32) * s}
    _L0_ffn_all = _L0_ffn_setup()
    _L0_ffn_in = {k: v for k, v in _L0_ffn_all.items() if k in ('gate_w', 'w_gate', 'w_up', 'w_down')}
    del _L0_ffn_all
    return {'x': x, 'ctx_512': ctx_512, 'L0_xattn_Wq': _L0_xattn_in['Wq'], 'L0_xattn_Wk': _L0_xattn_in['Wk'], 'L0_xattn_gamma_raw': _L0_xattn_in['gamma_raw'], 'L0_ffn_gate_w': _L0_ffn_in['gate_w'], 'L0_ffn_w_gate': _L0_ffn_in['w_gate'], 'L0_ffn_w_up': _L0_ffn_in['w_up'], 'L0_ffn_w_down': _L0_ffn_in['w_down']}

def reference(x, ctx_512, L0_xattn_Wq, L0_xattn_Wk, L0_xattn_gamma_raw, L0_ffn_gate_w, L0_ffn_w_gate, L0_ffn_w_up, L0_ffn_w_down):
    import jax
    import jax.numpy as jnp

    def _L0_xattn_ref(h, adj_raw, Wq, Wk, gamma_raw):
        import jax, jax.numpy as jnp
        import numpy as np
        B, N, D = (16, 256, 64)
        H = 4
        TOP_K_RATIO = 0.3
        b, n, dm = h.shape
        d = dm // H
        Q = (h @ Wq.T).reshape(b, n, H, d).transpose(0, 2, 1, 3)
        K = (h @ Wk.T).reshape(b, n, H, d).transpose(0, 2, 1, 3)
        sim = jnp.einsum('bhnd,bhmd->bnm', Q, K) / (jnp.sqrt(jnp.float32(d)) * H)
        k = max(1, int(n * TOP_K_RATIO))
        topk_vals = jax.lax.top_k(sim, k)[0]
        threshold = topk_vals[:, :, -1:]
        sparse_mask = (sim >= threshold).astype(sim.dtype)
        A_learned = jax.nn.sigmoid(sim) * sparse_mask
        A_learned = (A_learned + jnp.swapaxes(A_learned, -1, -2)) * 0.5
        gamma = jax.nn.sigmoid(gamma_raw)
        return (1.0 - gamma) * adj_raw + gamma * A_learned

    def _L0_ffn_ref(hidden_states, gate_w, w_gate, w_up, w_down):
        import jax, jax.numpy as jnp
        import numpy as np
        B, S, D, FF, E = (4, 256, 256, 1024, 2)
        b, s, d = hidden_states.shape
        x = hidden_states.reshape(-1, d)
        logits = x @ gate_w.T
        probs = jax.nn.softmax(logits.astype(jnp.float32), axis=-1)
        sel = jnp.argmax(probs, axis=-1)
        top_w = jnp.take_along_axis(probs, sel[:, None], axis=-1)
        onehot = jax.nn.one_hot(sel, gate_w.shape[0], dtype=x.dtype)
        g = jnp.einsum('td,efd->etf', x, w_gate)
        u = jnp.einsum('td,efd->etf', x, w_up)
        h = jax.nn.silu(g) * u
        y = jnp.einsum('etf,edf->etd', h, w_down)
        out = jnp.einsum('etd,te->td', y, onehot * top_w)
        return out.reshape(b, s, d)
    x = x + _L0_xattn_ref(ctx_512, _layernorm(x, axis=-1), L0_xattn_Wq, L0_xattn_Wk, L0_xattn_gamma_raw)
    x = x + _L0_ffn_ref(_layernorm(x, axis=-1), L0_ffn_gate_w, L0_ffn_w_gate, L0_ffn_w_up, L0_ffn_w_down)
    return x

_drawn_inputs = setup_inputs


def setup_inputs(seed=0):
    import zlib

    import numpy as np

    out = dict(_drawn_inputs(seed))
    spreads = {}
    factors = {'L0_ffn_gate_w': 4.402,
     'L0_ffn_w_gate': 3.235,
     'L0_ffn_w_up': 3.203,
     'L0_ffn_w_down': 3.204}
    for name, (base, spread) in spreads.items():
        noise = np.random.default_rng([zlib.crc32(name.encode()), seed]).standard_normal(out[name].shape)
        drawn = base * np.exp(spread * noise) if base else spread * noise
        out[name] = jnp.asarray(drawn.astype(out[name].dtype))
    for name, factor in factors.items():
        out[name] = (out[name] * factor).astype(out[name].dtype)
    return out
```

```python
from contextlib import ExitStack

import concourse.bass as bass
from concourse import mybir

ALU = mybir.AluOpType
ACT = mybir.ActivationFunctionType
F32 = mybir.dt.float32
F32R = mybir.dt.float32r

P = 128
EPS = 1e-5
LOWEST = -3.4028234e38
TOPK_RATIO = 0.3
HEADS = 4



def xattn_ffn_kernel(nc, x, ctx_t, wq_t, wk_t, gamma_raw, gate_w, w_gate_up, w_down, out):
    TOK, D = x.shape
    C = ctx_t.shape[0]
    KD = D // P
    CH = w_down.shape[1]
    E = gate_w.shape[0]
    CHE = CH // E
    N = D
    B = TOK // N
    R = N // P
    K = max(1, int(N * TOPK_RATIO))
    ROUNDS = -(-K // 8)
    KTH = (K - 1) % 8
    SIM_SCALE = 1.0 / ((C // HEADS) ** 0.5 * HEADS)
    RING = 4
    LAG = RING - 1
    PAIRS = CH // 2
    STAGE = 4
    PAIRS_AHEAD = 4
    assert R == 2 and KD == 2 and E == 2 and CH % RING == 0 and KTH == (K - 1) % 8

    x_tiles = x.rearrange("(t p) d -> p t d", p=P)
    out_tiles = out.rearrange("(t p) d -> p t d", p=P)

    with ExitStack() as stack:
        def sb(name, shape, dt=F32):
            return stack.enter_context(nc.sbuf_tensor(name, shape, dt))

        def pb(name, shape):
            return stack.enter_context(nc.psum_tensor(name, shape, F32))

        def sem(name):
            return stack.enter_context(nc.semaphore(name))

        stream = sb("stream", [P, B * R, D])
        ctx_sb = sb("ctx_sb", [C, TOK])
        wqk_sb = sb("wqk_sb", [C, 2, C])
        qk_sb = sb("qk_sb", [C, 2, TOK])
        gamma_in = sb("gamma_in", [P, 1])
        gamma_th = sb("gamma_th", [P, 1])
        keep = sb("keep", [P, 1])
        quarter = sb("quarter", [P, 1])
        gate_sb = sb("gate_sb", [P, E, D])
        gate_prod = sb("gate_prod", [P, D])
        stage_gu = sb("stage_gu", [P, STAGE, 2, 2 * KD * P])
        stage_d = sb("stage_d", [P, PAIRS, 2, D])
        gu_hi = sb("gu_hi", [P, CH, 2, KD, P], F32R)
        gu_lo = sb("gu_lo", [P, CH, 2, KD, P], F32R)
        d_hi = sb("d_hi", [P, CH, D], F32R)
        d_lo = sb("d_lo", [P, CH, D], F32R)
        sim = sb("sim", [P, B * R, N])
        left = sb("left", [P, R, N])
        top8 = sb("top8", [P, 2, R, 8])
        sig2 = sb("sig2", [P, R, N])
        kept2 = sb("kept2", [P, R, N])
        xn = sb("xn", [P, R, D])
        stat1 = sb("stat1", [P, B * R, 6])
        mv1 = sb("mv1", [P, B * R, 2])
        ve1 = sb("ve1", [P, B * R])
        rstd1 = sb("rstd1", [P, B * R])
        a1 = sb("a1", [P, B * R])
        s1 = sb("s1", [P, B * R])
        b1 = sb("b1", [P, B * R])
        stat2 = sb("stat2", [P, R, 6])
        mv2 = sb("mv2", [P, R, 2])
        ve2 = sb("ve2", [P, R])
        rstd2 = sb("rstd2", [P, R])
        minus_half = sb("minus_half", [P, B * R])
        eps = sb("eps", [P, R])
        ident = sb("ident", [P, P])
        xt_hi = sb("xt_hi", [P, B, KD * N], F32R)
        xt_lo = sb("xt_lo", [P, B, KD * N], F32R)
        logits = sb("logits", [P, R, E])
        margin = sb("margin", [P, R])
        tanh_m = sb("tanh_m", [P, R])
        prob = sb("prob", [P, E, R])
        chosen = sb("chosen", [P, E, R])
        weight = sb("weight", [P, B * R, E])
        silu = sb("silu", [P, 2, N])
        h = sb("h", [P, RING, N])
        h_hi = sb("h_hi", [P, RING, N], F32R)
        h_lo = sb("h_lo", [P, RING, N], F32R)

        gu_ps = [pb(f"gu_ps{i}", [P, 2, N]) for i in range(RING)]
        y_ps = [pb(f"y_ps{e}", [P, R, D]) for e in range(E)]
        mix_ps = pb("mix_ps", [P, R, N])
        xt_ps = pb("xt_ps", [P, KD, N])

        ctx_in, wqk_in, x_in, small_in = sem("ctx_in"), sem("wqk_in"), sem("x_in"), sem("small_in")
        ctx_rest_in = sem("ctx_rest_in")
        x_rest_in = sem("x_rest_in")
        w_in = [sem(f"w_in{i}") for i in range(PAIRS)]
        qk_ready, sim_ready, mixed_ready = sem("qk_ready"), sem("sim_ready"), sem("mixed_ready")
        xt_ready, gu_ready = sem("xt_ready"), sem("gu_ready")
        y_ready = [sem(f"y_ready{e}") for e in range(E)]
        gamma_ready, qk_copied, sim_copied = sem("gamma_ready"), sem("qk_copied"), sem("sim_copied")
        left_ready, sig_raw, sig_ready, ln_mixed = sem("left_ready"), sem("sig_raw"), sem("sig_ready"), sem("ln_mixed")
        w_hi_ready, xt_hi_ready, tanh_ready = sem("w_hi_ready"), sem("xt_hi_ready"), sem("tanh_ready")
        silu_ready, h_hi_ready = sem("silu_ready"), sem("h_hi_ready")
        vector_step, stats1_ready, ln1_ready = sem("vector_step"), sem("stats1_ready"), sem("ln1_ready")
        ranked, kept_ready, stats2_ready = sem("ranked"), sem("kept_ready"), sem("stats2_ready")
        xn_ready, xt_lo_ready, logits_ready = sem("xn_ready"), sem("xt_lo_ready"), sem("logits_ready")
        h_ready, y_free = sem("h_ready"), [sem(f"y_free{e}") for e in range(E)]
        const_step, const_ready, w_lo_ready = sem("const_step"), sem("const_ready"), sem("w_lo_ready")
        pool_step, rstd1_ready, rstd2_ready = sem("pool_step"), sem("rstd1_ready"), sem("rstd2_ready")
        h_lo_ready, margin_ready, weight_ready = sem("h_lo_ready"), sem("margin_ready"), sem("weight_ready")
        out_stored = sem("out_stored")

        def tiles(ap, t):
            return ap[:, bass.ds(R * t, R), :]

        block = stack.enter_context(nc.Block())

        @block.sync
        def _(sp):
            sp.dma_start(ctx_sb[:, 0:N], ctx_t[:, 0:N]).then_inc(ctx_in, 16)
            sp.dma_start(wqk_sb[:, 0, :], wq_t).then_inc(wqk_in, 16)
            sp.dma_start(wqk_sb[:, 1, :], wk_t).then_inc(wqk_in, 16)
            sp.dma_start(stream[:, 0:R, :], x_tiles[:, 0:R, :]).then_inc(x_in, 16)
            sp.dma_start(gamma_in[:, :], gamma_raw.partition_broadcast(P)).then_inc(small_in, 16)
            sp.dma_start(gate_sb[:, :, :], gate_w.partition_broadcast(P)).then_inc(small_in, 16)
            for i in range(PAIRS):
                if i == 1:
                    sp.dma_start(stream[:, R:, :], x_tiles[:, R:, :]).then_inc(x_rest_in, 16)
                    sp.dma_start(ctx_sb[:, N:], ctx_t[:, N:]).then_inc(ctx_rest_in, 16)
                if i >= STAGE:
                    sp.wait_ge(w_lo_ready, i - STAGE + 1)
                sp.dma_start(stage_gu[:, i % STAGE, :, :],
                             w_gate_up[:, 2 * i:2 * i + 2, :]).then_inc(w_in[i], 16)
                sp.dma_start(stage_d[:, i, :, :], w_down[:, 2 * i:2 * i + 2, :]).then_inc(w_in[i], 16)
            with sp.Fori(0, B) as b:
                sp.wait_ge(y_free[E - 1], b + 2)
                sp.dma_start(tiles(out_tiles, b), tiles(stream, b)).then_inc(out_stored, 16)
            sp.wait_ge(out_stored, 16 * B)

        @block.tensor
        def _(pe):
            def project(t):
                if t == 0:
                    pe.wait_ge(ctx_in, 16)
                    pe.wait_ge(wqk_in, 32)
                if t == 1:
                    pe.wait_ge(ctx_rest_in, 16)
                for i in range(2):
                    mm = pe.matmul(gu_ps[t % 2][0:C, i, :], wqk_sb[:, i, :], ctx_sb[:, N * t:N * (t + 1)],
                                   start=True, stop=True)
                mm.then_inc(qk_ready, 1)
                pe.wait_ge(qk_copied, t + 1)
                if t >= 2:
                    pe.wait_ge(sim_copied, t - 1)
                for r in range(R):
                    lo = N * t + P * r
                    mm = pe.matmul(gu_ps[2 + t % 2][:, r, :], qk_sb[:, 0, lo:lo + P],
                                   qk_sb[:, 1, N * t:N * (t + 1)], start=True, stop=True)
                mm.then_inc(sim_ready, 1)

            def transpose_kept(t):
                pe.wait_ge(kept_ready, t + 1)
                for r in range(R):
                    for s in range(R):
                        mm = pe.transpose(mix_ps[:, r, P * s:P * (s + 1)], kept2[:, s, P * r:P * (r + 1)], ident[:, :])
                mm.then_inc(mixed_ready, 1)

            def transpose_xn(t):
                pe.wait_ge(xn_ready, t + 1)
                for k in range(KD):
                    for r in range(R):
                        mm = pe.transpose(xt_ps[:, k, P * r:P * (r + 1)], xn[:, r, P * k:P * (k + 1)], ident[:, :])
                mm.then_inc(xt_ready, 1)

            def up(b, c):
                pe.wait_ge(w_lo_ready, c // 2 + 1)
                if c == 0:
                    pe.wait_ge(xt_lo_ready, b + 1)
                for j in range(2):
                    n = 0
                    for k in range(KD):
                        for w, xt in ((gu_hi, xt_hi), (gu_hi, xt_lo), (gu_lo, xt_hi)):
                            mm = pe.matmul(gu_ps[c % RING][:, j, :], w[:, c, j, k, :],
                                           xt[:, b, k * N:(k + 1) * N],
                                           start=(n == 0), stop=(n == 3 * KD - 1))
                            n += 1
                mm.then_inc(gu_ready, 1)

            def down(b, c):
                e = c // CHE
                if c % CHE == 0:
                    pe.wait_ge(y_free[e], b + 1)
                pe.wait_ge(h_lo_ready, CH * b + c + 1)
                for r in range(R):
                    for i, (a, w) in enumerate(((h_hi, d_hi), (h_hi, d_lo), (h_lo, d_hi))):
                        mm = pe.matmul(y_ps[e][:, r, :], a[:, c % RING, P * r:P * (r + 1)], w[:, c, :],
                                       start=(c % CHE == 0 and r == 0 and i == 0),
                                       stop=(c % CHE == CHE - 1 and i == 2), skip_group_check=True)
                if c % CHE == CHE - 1:
                    mm.then_inc(y_ready[e], 1)

            for t in range(B):
                project(t)
            pe.wait_ge(const_ready, 1)
            transpose_kept(0)
            transpose_xn(0)
            for c in range(LAG):
                up(0, c)
            with pe.Fori(0, B - 1) as b:
                for c in range(LAG, CH):
                    up(b, c)
                    down(b, c - LAG)
                    if c == 13:
                        transpose_kept(b + 1)
                transpose_xn(b + 1)
                for c in range(LAG):
                    up(b + 1, c)
                    down(b, CH - LAG + c)
            for c in range(LAG, CH):
                up(B - 1, c)
                down(B - 1, c - LAG)
            for c in range(CH - LAG, CH):
                down(B - 1, c)

        @block.scalar
        def _(act):
            act.preload_act_table(ACT.Silu)
            act.wait_ge(small_in, 32)
            nc.scalar.activation(gamma_th[:, :], gamma_in[:, :], ACT.Tanh, scale=0.5).then_inc(gamma_ready, 1)

            def copy_projections(t):
                act.wait_ge(qk_ready, t + 1)
                nc.scalar.copy(qk_sb[:, :, N * t:N * (t + 1)], gu_ps[t % 2][0:C, :, :]).then_inc(qk_copied, 1)
                act.wait_ge(sim_ready, t + 1)
                nc.scalar.copy(sim[:, R * t:R * (t + 1), :], gu_ps[2 + t % 2][:, :, :]).then_inc(sim_copied, 1)

            def sigmoid2(t):
                nc.scalar.activation(sig2[:, :, :], tiles(sim, t), ACT.Tanh, scale=0.5 * SIM_SCALE).then_inc(sig_raw, 1)
                act.wait_ge(sig_raw, t + 1)
                nc.scalar.add(sig2[:, :, :], sig2[:, :, :], 1.0).then_inc(sig_ready, 1)

            def mix_ln1(t, r):
                i = R * t + r
                ins = nc.scalar.activation(stream[:, i, :], stream[:, i, :], ACT.Identity,
                                           scale=s1[:, bass.ds(i, 1)], bias=b1[:, bass.ds(i, 1)])
                if r == R - 1:
                    ins.then_inc(ln_mixed, 1)

            def split_weights(i):
                act.wait_ge(w_in[i], 32)
                nc.scalar.copy(gu_hi[:, 2 * i:2 * i + 2, :, :, :].rearrange("p c j k f -> p c (j k f)"),
                               stage_gu[:, i % STAGE, :, :]).then_inc(w_hi_ready, 1)
                nc.scalar.copy(d_hi[:, 2 * i:2 * i + 2, :], stage_d[:, i, :, :]).then_inc(w_hi_ready, 1)

            def transpose_hi(t):
                nc.scalar.copy(xt_hi[:, t, :], xt_ps[:, :, :].rearrange("p k n -> p (k n)")).then_inc(xt_hi_ready, 1)

            def gate_tanh(t):
                act.wait_ge(margin_ready, t + 1)
                nc.scalar.activation(tanh_m[:, :], margin[:, :], ACT.Tanh, scale=0.5).then_inc(tanh_ready, 1)

            def silu_of(b, c):
                act.wait_ge(gu_ready, CH * b + c + 1)
                nc.scalar.activation(silu[:, c % 2, :], gu_ps[c % RING][:, 0, :], ACT.Silu).then_inc(silu_ready, 1)

            def split_h(b, c):
                act.wait_ge(h_ready, CH * b + c + 1)
                nc.scalar.copy(h_hi[:, c % RING, :], h[:, c % RING, :]).then_inc(h_hi_ready, 1)

            copy_projections(0)
            act.wait_ge(sim_copied, 1)
            sigmoid2(0)
            for t in range(1, B):
                split_weights(t - 1)
                copy_projections(t)
            for i in range(B - 1, PAIRS):
                if i == B:
                    act.wait_ge(ln1_ready, 1)
                    mix_ln1(0, 0)
                    mix_ln1(0, 1)
                split_weights(i)
            act.wait_ge(xt_ready, 1)
            transpose_hi(0)
            silu_of(0, 0)
            with act.Fori(0, B - 1) as b:
                for c in range(1, CH):
                    silu_of(b, c)
                    if c == 1:
                        act.wait_ge(ranked, b + 1)
                    if c == 2:
                        act.wait_ge(kept_ready, b + 1)
                    split_h(b, c - 1)
                    if c == 1:
                        nc.scalar.copy(left[:, :, :], tiles(sim, b + 1)).then_inc(left_ready, 1)
                    if c == 2:
                        sigmoid2(b + 1)
                    if c == 3:
                        gate_tanh(b)
                    if c in (4, 5):
                        mix_ln1(b + 1, c - 4)
                act.wait_ge(xt_ready, b + 2)
                split_h(b, CH - 1)
                transpose_hi(b + 1)
                silu_of(b + 1, 0)
            for c in range(1, CH):
                silu_of(B - 1, c)
                split_h(B - 1, c - 1)
                if c == 3:
                    gate_tanh(B - 1)
            split_h(B - 1, CH - 1)

        @block.vector
        def _(dve):
            steps = [0]

            def step(ins):
                ins.then_inc(vector_step, 1)
                steps[0] += 1
                return steps[0]

            def restart():
                dve.wait_ge(vector_step, steps[0])
                dve.sem_clear(vector_step)
                steps[0] = 0

            def stats1(tile):
                n = step(nc.vector.bn_stats(stat1[:, tile, :], stream[:, tile, :]))
                return n

            def rank(n, first, found, removed):
                for r in range(R):
                    src = first[:, r, :] if n == 0 else left[:, r, :]
                    if n:
                        dve.wait_ge(vector_step, removed[r])
                    ins = nc.vector.max(top8[:, n % 2, r, :], src)
                    if n == ROUNDS - 1 and r == R - 1:
                        ins.then_inc(ranked, 1)
                    else:
                        found[r] = step(ins)
                if n == ROUNDS - 1:
                    return
                for r in range(R):
                    src = first[:, r, :] if n == 0 else left[:, r, :]
                    dve.wait_ge(vector_step, found[r])
                    removed[r] = step(nc.vector.match_replace(left[:, r, :], top8[:, n % 2, r, :], src, LOWEST))

            def keep_top(t):
                dve.wait_ge(ranked, t + 1)
                dve.wait_ge(sig_ready, t + 1)
                for r in range(R):
                    ins = nc.vector.scalar_tensor_tensor(
                        out=kept2[:, r, :], in0=sim[:, R * t + r, :],
                        scalar=top8[:, (ROUNDS - 1) % 2, r, KTH:KTH + 1], in1=sig2[:, r, :],
                        op0=ALU.is_ge, op1=ALU.mult)
                ins.then_inc(kept_ready, 1)

            def add_adjacency(t):
                dve.wait_ge(mixed_ready, t + 1)
                n = step(nc.vector.tensor_tensor(xn[:, :, :], mix_ps[:, :, :], kept2[:, :, :], ALU.add))
                dve.wait_ge(ln_mixed, t + 1)
                dve.wait_ge(vector_step, n)
                n = step(nc.vector.scalar_tensor_tensor(out=tiles(stream, t), in0=xn[:, :, :], scalar=quarter[:, 0:1],
                                                        in1=tiles(stream, t), op0=ALU.mult, op1=ALU.add))
                dve.wait_ge(vector_step, n)
                for r in range(R):
                    n = step(nc.vector.bn_stats(stat2[:, r, :], stream[:, R * t + r, :]))
                dve.wait_ge(vector_step, n - 1)
                nc.vector.bn_aggr(mv2[:, 0, :], stat2[:, 0, :]).then_inc(stats2_ready, 1)
                dve.wait_ge(vector_step, n)
                nc.vector.bn_aggr(mv2[:, 1, :], stat2[:, 1, :]).then_inc(stats2_ready, 1)

            def norm2(t):
                dve.wait_ge(rstd2_ready, t + 1)
                for r in range(R):
                    ins = nc.vector.tensor_scalar(xn[:, r, :], stream[:, R * t + r, :], mv2[:, r, 0:1],
                                                  rstd2[:, r:r + 1], ALU.subtract, ALU.mult)
                ins.then_inc(xn_ready, 1)

            def transpose_lo(t):
                dve.wait_ge(xt_hi_ready, t + 1)
                nc.vector.tensor_tensor(xt_lo[:, t, :], xt_ps[:, :, :].rearrange("p k n -> p (k n)"),
                                        xt_hi[:, t, :].bitcast(F32), ALU.subtract).then_inc(xt_lo_ready, 1)

            def gate(t):
                for r in range(R):
                    for e in range(E):
                        if r or e:
                            dve.wait_ge(vector_step, n)
                        ins = nc.vector.tensor_tensor_reduce(gate_prod[:, :], xn[:, r, :], gate_sb[:, e, :], 1.0, 0.0,
                                                             ALU.mult, ALU.add, logits[:, r, e:e + 1])
                        if r == R - 1 and e == E - 1:
                            ins.then_inc(logits_ready, 1)
                        else:
                            n = step(ins)

            def hidden(b, c):
                dve.wait_ge(silu_ready, CH * b + c + 1)
                nc.vector.tensor_tensor(h[:, c % RING, :], gu_ps[c % RING][:, 1, :], silu[:, c % 2, :],
                                        ALU.mult).then_inc(h_ready, 1)

            def add_expert(b, e):
                dve.wait_ge(y_ready[e], b + 1)
                if e == 0:
                    dve.wait_ge(weight_ready, b + 1)
                else:
                    dve.wait_ge(y_free[0], b + 2)
                for r in range(R):
                    i = R * b + r
                    ins = nc.vector.scalar_tensor_tensor(out=stream[:, i, :], in0=y_ps[e][:, r, :],
                                                         scalar=weight[:, i, e:e + 1], in1=stream[:, i, :],
                                                         op0=ALU.mult, op1=ALU.add)
                ins.then_inc(y_free[e], 1)

            for e in range(E):
                dve.sem_inc(y_free[e], 1)
            dve.wait_ge(small_in, 32)
            dve.wait_ge(gamma_ready, 1)
            nc.vector.tensor_scalar(quarter[:, :], gamma_th[:, :], 0.125, 0.125, ALU.mult, ALU.add)
            step(nc.vector.tensor_scalar(keep[:, :], gamma_th[:, :], -0.5, 0.5, ALU.mult, ALU.add))
            for i in range(B * R):
                if i == 0:
                    dve.wait_ge(x_in, 16)
                if i == R:
                    dve.wait_ge(x_rest_in, 16)
                n = stats1(i)
            dve.wait_ge(vector_step, n)
            for i in range(B * R):
                ins = nc.vector.bn_aggr(mv1[:, i, :], stat1[:, i, :])
            ins.then_inc(stats1_ready, 1)
            found, removed = [0, 0], [0, 0]
            dve.wait_ge(sim_copied, 1)
            for n in range(ROUNDS):
                rank(n, sim, found, removed)
                if n == 1:
                    dve.wait_ge(rstd1_ready, 1)
                    m = step(nc.vector.tensor_scalar(a1[:, :], rstd1[:, :], keep[:, 0:1], None, ALU.mult))
                if n == 2:
                    dve.wait_ge(vector_step, m)
                    step(nc.vector.tensor_scalar(s1[:, :], a1[:, :], 1.0, None, ALU.add))
                    nc.vector.scalar_tensor_tensor(out=b1[:, :], in0=mv1[:, :, 0], scalar=-1.0, in1=a1[:, :],
                                                   op0=ALU.mult, op1=ALU.mult).then_inc(ln1_ready, 1)
            keep_top(0)
            add_adjacency(0)
            norm2(0)
            transpose_lo(0)
            gate(0)
            restart()
            for c in range(LAG):
                hidden(0, c)
            with dve.Fori(0, B - 1) as b:
                found, removed = [0, 0], [0, 0]
                n = 0
                dve.wait_ge(left_ready, b + 1)
                for c in range(LAG, CH):
                    hidden(b, c)
                    for _ in range(2 if c in (3, 10) else 1 if c < 10 else 0):
                        rank(n, left, found, removed)
                        n += 1
                    if c == 11:
                        keep_top(b + 1)
                    if c == 12:
                        add_expert(b, 0)
                    if c == 13:
                        add_adjacency(b + 1)
                    if c == 14:
                        norm2(b + 1)
                transpose_lo(b + 1)
                gate(b + 1)
                for c in range(LAG):
                    hidden(b + 1, c)
                add_expert(b, 1)
                restart()
            for c in range(LAG, CH):
                hidden(B - 1, c)
                if c == 12:
                    add_expert(B - 1, 0)
            add_expert(B - 1, 1)

        @block.gpsimd
        def _(pool):
            def split_weights(i):
                pool.wait_ge(w_hi_ready, 2 * i + 2)
                nc.gpsimd.tensor_tensor(gu_lo[:, 2 * i:2 * i + 2, :, :, :].rearrange("p c j k f -> p c (j k f)"),
                                        stage_gu[:, i % STAGE, :, :],
                                        gu_hi[:, 2 * i:2 * i + 2, :, :, :].rearrange("p c j k f -> p c (j k f)").bitcast(F32),
                                        ALU.subtract)
                nc.gpsimd.tensor_tensor(d_lo[:, 2 * i:2 * i + 2, :], stage_d[:, i, :, :],
                                        d_hi[:, 2 * i:2 * i + 2, :].bitcast(F32), ALU.subtract).then_inc(w_lo_ready, 1)

            def split_h(b, c):
                pool.wait_ge(h_hi_ready, CH * b + c + 1)
                nc.gpsimd.tensor_tensor(h_lo[:, c % RING, :], h[:, c % RING, :], h_hi[:, c % RING, :].bitcast(F32),
                                        ALU.subtract).then_inc(h_lo_ready, 1)

            def rstd_of_x1(t):
                pool.wait_ge(stats2_ready, R * (t + 1))
                nc.gpsimd.tensor_tensor(ve2[:, :], mv2[:, :, 1], eps[:, :], ALU.add).then_inc(pool_step, 1)
                pool.wait_ge(pool_step, 1)
                nc.gpsimd.tensor_tensor(rstd2[:, :], ve2[:, :], minus_half[:, 0:R], ALU.pow).then_inc(rstd2_ready, 1)
                pool.sem_clear(pool_step)

            def gate_margin(t):
                pool.wait_ge(logits_ready, t + 1)
                nc.gpsimd.tensor_tensor(margin[:, :], logits[:, :, 0], logits[:, :, 1], ALU.subtract).then_inc(margin_ready, 1)

            def expert_weights(t):
                for e, (sign, wins) in enumerate(((0.5, ALU.is_ge), (-0.5, ALU.is_lt))):
                    nc.gpsimd.tensor_scalar(prob[:, e, :], tanh_m[:, :], sign, 0.5, ALU.mult, ALU.add).then_inc(pool_step, 1)
                    nc.gpsimd.tensor_scalar(chosen[:, e, :], tanh_m[:, :], 0.0, None, wins).then_inc(pool_step, 1)
                for e in range(E):
                    pool.wait_ge(pool_step, 2 * e + 2)
                    ins = nc.gpsimd.tensor_tensor(weight[:, bass.ds(R * t, R), e], prob[:, e, :], chosen[:, e, :], ALU.mult)
                ins.then_inc(weight_ready, 1)
                pool.sem_clear(pool_step)

            nc.gpsimd.memset(minus_half[:, :], -0.5)
            nc.gpsimd.memset(eps[:, :], EPS)
            nc.gpsimd.memset(ident[:, :], 0.0).then_inc(const_step, 1)
            pool.wait_ge(const_step, 1)
            nc.gpsimd.affine_select(out=ident[:, :], in_=ident[:, :], compare_op=ALU.not_equal, fill=1.0, base=0,
                                    pattern=[[-1, P]], channel_multiplier=1).then_inc(const_ready, 1)
            pool.wait_ge(stats1_ready, 1)
            nc.gpsimd.tensor_scalar(ve1[:, :], mv1[:, :, 1], EPS, None, ALU.add).then_inc(pool_step, 1)
            pool.wait_ge(pool_step, 1)
            nc.gpsimd.tensor_tensor(rstd1[:, :], ve1[:, :], minus_half[:, :], ALU.pow).then_inc(rstd1_ready, 1)
            pool.sem_clear(pool_step)
            for i in range(PAIRS_AHEAD):
                split_weights(i)
            rstd_of_x1(0)
            for c in range(CH):
                if c == 3:
                    pool.wait_ge(tanh_ready, 1)
                split_h(0, c)
                if c % 2 == 0 and PAIRS_AHEAD + c // 2 < PAIRS:
                    split_weights(PAIRS_AHEAD + c // 2)
                if c == 1:
                    gate_margin(0)
                if c == 3:
                    expert_weights(0)
                if c == 13:
                    rstd_of_x1(1)
            with pool.Fori(1, B - 1) as b:
                for c in range(CH):
                    if c == 3:
                        pool.wait_ge(tanh_ready, b + 1)
                    split_h(b, c)
                    if c == 1:
                        gate_margin(b)
                    if c == 3:
                        expert_weights(b)
                    if c == 13:
                        rstd_of_x1(b + 1)
            for c in range(CH):
                if c == 3:
                    pool.wait_ge(tanh_ready, B)
                split_h(B - 1, c)
                if c == 1:
                    gate_margin(B - 1)
                if c == 3:
                    expert_weights(B - 1)


def kernel(x, ctx_512, L0_xattn_Wq, L0_xattn_Wk, L0_xattn_gamma_raw, L0_ffn_gate_w, L0_ffn_w_gate, L0_ffn_w_up, L0_ffn_w_down):
    import numpy as np
    import concourse.bacc as bacc
    from concourse.bass_utils import run_bass_kernel_spmd

    B, N, D = x.shape
    E, F, _ = L0_ffn_w_gate.shape
    blocks = [np.asarray(w).reshape(E * F // P, P, D // P, P).transpose(3, 0, 2, 1) for w in (L0_ffn_w_gate, L0_ffn_w_up)]
    down = np.asarray(L0_ffn_w_down).reshape(E, D, F // P, P).transpose(3, 0, 2, 1)
    arrays = {
        "x": np.asarray(x).reshape(B * N, D),
        "ctx_t": np.asarray(ctx_512).reshape(B * N, -1).T,
        "wq_t": np.asarray(L0_xattn_Wq).T,
        "wk_t": np.asarray(L0_xattn_Wk).T,
        "gamma_raw": np.asarray(L0_xattn_gamma_raw).reshape(1),
        "gate_w": np.asarray(L0_ffn_gate_w),
        "w_gate_up": np.stack(blocks, axis=2).reshape(P, E * F // P, 2 * D),
        "w_down": down.reshape(P, E * F // P, D),
    }
    arrays = {name: np.ascontiguousarray(a) for name, a in arrays.items()}
    nc = bacc.Bacc("TRN2", target_bir_lowering=False, num_devices=1)
    aps = [nc.dram_tensor(f"{name}_dram", a.shape, mybir.dt.from_np(a.dtype), kind="ExternalInput").ap()
           for name, a in arrays.items()]
    out = nc.dram_tensor("out_dram", (B * N, D), F32, kind="ExternalOutput").ap()
    xattn_ffn_kernel(nc, *aps, out)
    got = run_bass_kernel_spmd(nc, [{f"{name}_dram": a for name, a in arrays.items()}], core_ids=[0])
    return got.results[0]["out_dram"].reshape(B, N, D)
```

```python
from contextlib import ExitStack

import concourse.bass as bass
from concourse import mybir

ALU = mybir.AluOpType
ACT = mybir.ActivationFunctionType
F32 = mybir.dt.float32
F32R = mybir.dt.float32r

P = 128
EPS = 1e-5
LOWEST = -3.4028234e38
TOPK_RATIO = 0.3
HEADS = 4



def xattn_ffn_kernel(nc, x, ctx_t, wqk_t, gamma_raw, gate_w, w_gate_up, w_down, out):
    TOK, D = x.shape
    C = ctx_t.shape[0]
    KD = D // P
    CH = w_down.shape[1]
    E = gate_w.shape[0]
    CHE = CH // E
    N = D
    B = TOK // N
    R = N // P
    K = max(1, int(N * TOPK_RATIO))
    ROUNDS = -(-K // 8)
    KTH = (K - 1) % 8
    SIM_SCALE = 1.0 / ((C // HEADS) ** 0.5 * HEADS)
    RING = 4
    LAG = RING - 1
    PAIRS = CH // 2
    STAGE = 7
    PAIRS_AHEAD = 5
    KEEP_AT = CH - 5
    RANKED_AT = [LAG, LAG, LAG + 1, LAG + 1] + list(range(LAG + 2, KEEP_AT))
    assert len(RANKED_AT) == ROUNDS
    assert R == 2 and KD == 2 and E == 2 and CH % RING == 0 and KTH == (K - 1) % 8

    x_tiles = x.rearrange("(t p) d -> p t d", p=P)
    out_tiles = out.rearrange("(t p) d -> p t d", p=P)

    with ExitStack() as stack:
        def sb(name, shape, dt=F32):
            return stack.enter_context(nc.sbuf_tensor(name, shape, dt))

        def pb(name, shape):
            return stack.enter_context(nc.psum_tensor(name, shape, F32))

        def sem(name):
            return stack.enter_context(nc.semaphore(name))

        stream = sb("stream", [P, B * R, D])
        ctx_sb = sb("ctx_sb", [C, TOK])
        wqk_sb = sb("wqk_sb", [C, 2, C])
        qk_sb = sb("qk_sb", [C, 2, 2, N])
        gamma_in = sb("gamma_in", [P, 1])
        gamma_th = sb("gamma_th", [P, 1])
        keep = sb("keep", [P, 1])
        quarter = sb("quarter", [P, 1])
        gate_sb = sb("gate_sb", [P, E, D])
        gate_prod = sb("gate_prod", [P, D])
        stage_gu = sb("stage_gu", [P, STAGE, 2, 2 * KD * P])
        stage_d = sb("stage_d", [P, PAIRS, 2, D])
        gu_hi = sb("gu_hi", [P, CH, 2, KD, P], F32R)
        gu_lo = sb("gu_lo", [P, CH, 2, KD, P], F32R)
        d_hi = sb("d_hi", [P, CH, D], F32R)
        d_lo = sb("d_lo", [P, CH, D], F32R)
        sim = sb("sim", [P, B * R, N])
        left = sb("left", [P, R, N])
        top8 = sb("top8", [P, 2, R, 8])
        sig2 = sb("sig2", [P, R, N])
        kept2 = sb("kept2", [P, R, N])
        xn = sb("xn", [P, R, D])
        stat1 = sb("stat1", [P, B * R, 6])
        mv1 = sb("mv1", [P, B * R, 2])
        ve1 = sb("ve1", [P, B * R])
        rstd1 = sb("rstd1", [P, B * R])
        a1 = sb("a1", [P, B * R])
        s1 = sb("s1", [P, B * R])
        b1 = sb("b1", [P, B * R])
        stat2 = sb("stat2", [P, R, 6])
        mv2 = sb("mv2", [P, R, 2])
        ve2 = sb("ve2", [P, R])
        rstd2 = sb("rstd2", [P, R])
        minus_half = sb("minus_half", [P, B * R])
        eps = sb("eps", [P, R])
        ident = sb("ident", [P, P])
        xt_hi = sb("xt_hi", [P, B, KD * N], F32R)
        xt_lo = sb("xt_lo", [P, B, KD * N], F32R)
        logits = sb("logits", [P, R, E])
        margin = sb("margin", [P, R])
        tanh_m = sb("tanh_m", [P, R])
        prob = sb("prob", [P, E, R])
        chosen = sb("chosen", [P, E, R])
        weight = sb("weight", [P, B * R, E])
        silu = sb("silu", [P, 2, N])
        h = sb("h", [P, RING, N])
        h_hi = sb("h_hi", [P, RING, N], F32R)
        h_lo = sb("h_lo", [P, RING, N], F32R)

        gu_ps = [pb(f"gu_ps{i}", [P, 2, N]) for i in range(RING)]
        y_ps = [pb(f"y_ps{e}", [P, R, D]) for e in range(E)]
        mix_ps = pb("mix_ps", [P, R, N])
        xt_ps = pb("xt_ps", [P, KD, N])

        ctx_in, wqk_in, x_in, gate_in = sem("ctx_in"), sem("wqk_in"), sem("x_in"), sem("gate_in")
        gamma_landed = sem("gamma_landed")
        ctx_rest_in = sem("ctx_rest_in")
        x_rest_in = sem("x_rest_in")
        w_in = [sem(f"w_in{i}") for i in range(PAIRS)]
        q_ready, k_ready, sim_ready, mixed_ready = sem("q_ready"), sem("k_ready"), sem("sim_ready"), sem("mixed_ready")
        xt_ready, gu_ready = sem("xt_ready"), sem("gu_ready")
        y_ready = [sem(f"y_ready{e}") for e in range(E)]
        gamma_ready, q_copied, k_copied, sim_copied = sem("gamma_ready"), sem("q_copied"), sem("k_copied"), sem("sim_copied")
        left_ready, sig_raw, sig_ready, ln_mixed = sem("left_ready"), sem("sig_raw"), sem("sig_ready"), sem("ln_mixed")
        w_hi_ready, xt_hi_ready, tanh_ready = sem("w_hi_ready"), sem("xt_hi_ready"), sem("tanh_ready")
        silu_ready, h_hi_ready = sem("silu_ready"), sem("h_hi_ready")
        first_k_copied = sem("first_k_copied")
        vector_step, stats1_ready, ln1_ready = sem("vector_step"), sem("stats1_ready"), sem("ln1_ready")
        ranked, kept_ready, stats2_ready = sem("ranked"), sem("kept_ready"), sem("stats2_ready")
        xn_ready, xt_lo_ready, logits_ready = sem("xn_ready"), sem("xt_lo_ready"), sem("logits_ready")
        h_ready, y_free = sem("h_ready"), [sem(f"y_free{e}") for e in range(E)]
        out_ready = sem("out_ready")
        const_step, const_ready, w_lo_ready = sem("const_step"), sem("const_ready"), sem("w_lo_ready")
        pool_step, rstd1_ready, rstd2_ready = sem("pool_step"), sem("rstd1_ready"), sem("rstd2_ready")
        h_lo_ready, margin_ready, weight_ready = sem("h_lo_ready"), sem("margin_ready"), sem("weight_ready")
        out_stored = sem("out_stored")

        def tiles(ap, t):
            return ap[:, bass.ds(R * t, R), :]

        block = stack.enter_context(nc.Block())

        @block.sync
        def _(sp):
            sp.dma_start(ctx_sb[:, 0:N], ctx_t[:, 0:N]).then_inc(ctx_in, 16)
            sp.dma_start(stream[:, 0:R, :], x_tiles[:, 0:R, :]).then_inc(x_in, 16)
            for i in range(PAIRS):
                if i == 1:
                    sp.dma_start(ctx_sb[:, N:], ctx_t[:, N:]).then_inc(ctx_rest_in, 16)
                if i == 2:
                    sp.dma_start(stream[:, R:, :], x_tiles[:, R:, :]).then_inc(x_rest_in, 16)
                if i >= STAGE:
                    sp.wait_ge(w_lo_ready, i - STAGE + 1)
                sp.dma_start(stage_gu[:, i % STAGE, :, :],
                             w_gate_up[:, 2 * i:2 * i + 2, :]).then_inc(w_in[i], 16)
                sp.dma_start(stage_d[:, i, :, :], w_down[:, 2 * i:2 * i + 2, :]).then_inc(w_in[i], 16)
            with sp.Fori(0, B * R) as i:
                sp.wait_ge(out_ready, i + 1)
                sp.dma_start(out_tiles[:, i, :], stream[:, i, :]).then_inc(out_stored, 16)
            sp.wait_ge(out_stored, 16 * B * R)

        @block.tensor
        def _(pe):
            def project(t):
                if t == 0:
                    pe.wait_ge(ctx_in, 16)
                    pe.wait_ge(wqk_in, 16)
                if t == 1:
                    pe.wait_ge(ctx_rest_in, 16)
                for i, ready in enumerate((q_ready, k_ready)):
                    pe.matmul(gu_ps[i][0:C, 0, :], wqk_sb[:, i, :], ctx_sb[:, N * t:N * (t + 1)],
                              start=True, stop=True).then_inc(ready, 1)
                pe.wait_ge(q_copied, t + 1)
                if t:
                    pe.wait_ge(k_copied, t)
                    pe.wait_ge(sim_copied, R * t)
                else:
                    pe.wait_ge(first_k_copied, 1)
                for r in range(R):
                    pe.matmul(gu_ps[2 + r][:, 0, :], qk_sb[:, t % 2, 0, P * r:P * (r + 1)], qk_sb[:, t % 2, 1, :],
                              start=True, stop=True).then_inc(sim_ready, 1)

            def transpose_kept(t):
                pe.wait_ge(kept_ready, t + 1)
                for r in range(R):
                    for s in range(R):
                        mm = pe.transpose(mix_ps[:, r, P * s:P * (s + 1)], kept2[:, s, P * r:P * (r + 1)], ident[:, :])
                mm.then_inc(mixed_ready, 1)

            def transpose_xn(t):
                pe.wait_ge(xn_ready, t + 1)
                for k in range(KD):
                    for r in range(R):
                        mm = pe.transpose(xt_ps[:, k, P * r:P * (r + 1)], xn[:, r, P * k:P * (k + 1)], ident[:, :])
                mm.then_inc(xt_ready, 1)

            def up(b, c):
                pe.wait_ge(w_lo_ready, c // 2 + 1)
                if c == 0:
                    pe.wait_ge(xt_lo_ready, b + 1)
                for j in range(2):
                    n = 0
                    for k in range(KD):
                        for w, xt in ((gu_hi, xt_hi), (gu_hi, xt_lo), (gu_lo, xt_hi)):
                            mm = pe.matmul(gu_ps[c % RING][:, j, :], w[:, c, j, k, :],
                                           xt[:, b, k * N:(k + 1) * N],
                                           start=(n == 0), stop=(n == 3 * KD - 1))
                            n += 1
                mm.then_inc(gu_ready, 1)

            def down(b, c):
                e = c // CHE
                if c % CHE == 0:
                    pe.wait_ge(y_free[e], b + 1)
                pe.wait_ge(h_lo_ready, CH * b + c + 1)
                for r in range(R):
                    for i, (a, w) in enumerate(((h_hi, d_hi), (h_hi, d_lo), (h_lo, d_hi))):
                        mm = pe.matmul(y_ps[e][:, r, :], a[:, c % RING, P * r:P * (r + 1)], w[:, c, :],
                                       start=(c % CHE == 0 and r == 0 and i == 0),
                                       stop=(c % CHE == CHE - 1 and i == 2), skip_group_check=True)
                if c % CHE == CHE - 1:
                    mm.then_inc(y_ready[e], 1)

            for t in range(B):
                project(t)
            pe.wait_ge(const_ready, 1)
            transpose_kept(0)
            transpose_xn(0)
            for c in range(LAG):
                up(0, c)
            with pe.Fori(0, B - 1) as b:
                for c in range(LAG, CH):
                    up(b, c)
                    down(b, c - LAG)
                    if c == KEEP_AT + 1:
                        transpose_kept(b + 1)
                    if c == KEEP_AT + 3:
                        transpose_xn(b + 1)
                for c in range(LAG):
                    up(b + 1, c)
                    down(b, CH - LAG + c)
            for c in range(LAG, CH):
                up(B - 1, c)
                down(B - 1, c - LAG)
            for c in range(CH - LAG, CH):
                down(B - 1, c)

        @block.scalar
        def _(act):
            act.dma_start(wqk_sb[:, :, :], wqk_t).then_inc(wqk_in, 16)
            act.dma_start(gamma_in[:, :], gamma_raw.partition_broadcast(P)).then_inc(gamma_landed, 16)
            act.preload_act_table(ACT.Silu)
            act.wait_ge(gamma_landed, 16)
            nc.scalar.activation(gamma_th[:, :], gamma_in[:, :], ACT.Tanh, scale=0.5).then_inc(gamma_ready, 1)

            def copy_projections(t):
                act.wait_ge(q_ready, t + 1)
                nc.scalar.copy(qk_sb[:, t % 2, 0, :], gu_ps[0][0:C, 0, :]).then_inc(q_copied, 1)
                if t:
                    act.wait_ge(k_ready, t + 1)
                    nc.scalar.copy(qk_sb[:, t % 2, 1, :], gu_ps[1][0:C, 0, :]).then_inc(k_copied, 1)

            def copy_sim(t):
                for r in range(R):
                    act.wait_ge(sim_ready, R * t + r + 1)
                    nc.scalar.copy(sim[:, R * t + r, :], gu_ps[2 + r][:, 0, :]).then_inc(sim_copied, 1)

            def sigmoid2(t):
                nc.scalar.activation(sig2[:, :, :], tiles(sim, t), ACT.Tanh, scale=0.5 * SIM_SCALE).then_inc(sig_raw, 1)
                act.wait_ge(sig_raw, t + 1)
                nc.scalar.add(sig2[:, :, :], sig2[:, :, :], 1.0).then_inc(sig_ready, 1)

            def mix_ln1(t, r):
                i = R * t + r
                ins = nc.scalar.activation(stream[:, i, :], stream[:, i, :], ACT.Identity,
                                           scale=s1[:, bass.ds(i, 1)], bias=b1[:, bass.ds(i, 1)])
                if r == R - 1:
                    ins.then_inc(ln_mixed, 1)

            def split_weights(i):
                act.wait_ge(w_in[i], 32)
                nc.scalar.copy(gu_hi[:, 2 * i:2 * i + 2, :, :, :].rearrange("p c j k f -> p c (j k f)"),
                               stage_gu[:, i % STAGE, :, :]).then_inc(w_hi_ready, 1)
                nc.scalar.copy(d_hi[:, 2 * i:2 * i + 2, :], stage_d[:, i, :, :]).then_inc(w_hi_ready, 1)

            def transpose_hi(t):
                nc.scalar.copy(xt_hi[:, t, :], xt_ps[:, :, :].rearrange("p k n -> p (k n)")).then_inc(xt_hi_ready, 1)

            def gate_tanh(t):
                act.wait_ge(margin_ready, t + 1)
                nc.scalar.activation(tanh_m[:, :], margin[:, :], ACT.Tanh, scale=0.5).then_inc(tanh_ready, 1)

            def silu_of(b, c):
                act.wait_ge(gu_ready, CH * b + c + 1)
                nc.scalar.activation(silu[:, c % 2, :], gu_ps[c % RING][:, 0, :], ACT.Silu).then_inc(silu_ready, 1)

            def split_h(b, c):
                act.wait_ge(h_ready, CH * b + c + 1)
                nc.scalar.copy(h_hi[:, c % RING, :], h[:, c % RING, :]).then_inc(h_hi_ready, 1)

            copy_projections(0)
            copy_sim(0)
            split_weights(0)
            act.wait_ge(sim_copied, R)
            sigmoid2(0)
            split_weights(1)
            act.wait_ge(ln1_ready, 1)
            mix_ln1(0, 0)
            mix_ln1(0, 1)
            for t in range(1, B):
                copy_projections(t)
                copy_sim(t)
                split_weights(t + 1)
            act.dma_start(gate_sb[:, :, :], gate_w.partition_broadcast(P)).then_inc(gate_in, 16)
            for i in range(B + 1, PAIRS - 1):
                split_weights(i)
            act.wait_ge(xt_ready, 1)
            transpose_hi(0)
            split_weights(PAIRS - 1)
            silu_of(0, 0)
            with act.Fori(0, B - 1) as b:
                for c in range(1, CH - 1):
                    silu_of(b, c)
                    if c == 1:
                        act.wait_ge(ranked, b + 1)
                    if c == 2:
                        act.wait_ge(kept_ready, b + 1)
                    split_h(b, c - 1)
                    if c == 1:
                        nc.scalar.copy(left[:, :, :], tiles(sim, b + 1)).then_inc(left_ready, 1)
                    if c == 2:
                        sigmoid2(b + 1)
                    if c == 3:
                        gate_tanh(b)
                    if c == 4:
                        act.wait_ge(ln1_ready, 2)
                    if c in (4, 5):
                        mix_ln1(b + 1, c - 4)
                act.wait_ge(xt_ready, b + 2)
                split_h(b, CH - 2)
                transpose_hi(b + 1)
                silu_of(b, CH - 1)
                split_h(b, CH - 1)
                silu_of(b + 1, 0)
            for c in range(1, CH):
                silu_of(B - 1, c)
                split_h(B - 1, c - 1)
                if c == 3:
                    gate_tanh(B - 1)
            split_h(B - 1, CH - 1)

        @block.vector
        def _(dve):
            steps = [0]

            def step(ins):
                ins.then_inc(vector_step, 1)
                steps[0] += 1
                return steps[0]

            def restart():
                dve.wait_ge(vector_step, steps[0])
                dve.sem_clear(vector_step)
                steps[0] = 0

            def stats1(first, end):
                for i in range(first, end):
                    step(nc.vector.bn_stats(stat1[:, i, :], stream[:, i, :]))

            def moments1(first, end):
                dve.wait_ge(vector_step, steps[0])
                for i in range(first, end):
                    ins = nc.vector.bn_aggr(mv1[:, i, :], stat1[:, i, :])
                ins.then_inc(stats1_ready, 1)

            def scale1(first, end):
                call = 1 if first == 0 else 2
                dve.wait_ge(rstd1_ready, call)
                n = step(nc.vector.tensor_scalar(a1[:, first:end], rstd1[:, first:end], keep[:, 0:1], None, ALU.mult))
                dve.wait_ge(vector_step, n)
                step(nc.vector.tensor_scalar(s1[:, first:end], a1[:, first:end], 1.0, None, ALU.add))
                nc.vector.scalar_tensor_tensor(out=b1[:, first:end], in0=mv1[:, first:end, 0], scalar=-1.0,
                                               in1=a1[:, first:end], op0=ALU.mult, op1=ALU.mult).then_inc(ln1_ready, 1)

            def rank(n, first, found, removed):
                for r in range(R):
                    src = first[:, r, :] if n == 0 else left[:, r, :]
                    if n:
                        dve.wait_ge(vector_step, removed[r])
                    elif first is sim:
                        dve.wait_ge(sim_copied, r + 1)
                    ins = nc.vector.max(top8[:, n % 2, r, :], src)
                    if n == ROUNDS - 1 and r == R - 1:
                        ins.then_inc(ranked, 1)
                    else:
                        found[r] = step(ins)
                if n == ROUNDS - 1:
                    return
                for r in range(R):
                    src = first[:, r, :] if n == 0 else left[:, r, :]
                    dve.wait_ge(vector_step, found[r])
                    removed[r] = step(nc.vector.match_replace(left[:, r, :], top8[:, n % 2, r, :], src, LOWEST))

            def keep_top(t):
                dve.wait_ge(ranked, t + 1)
                dve.wait_ge(sig_ready, t + 1)
                for r in range(R):
                    ins = nc.vector.scalar_tensor_tensor(
                        out=kept2[:, r, :], in0=sim[:, R * t + r, :],
                        scalar=top8[:, (ROUNDS - 1) % 2, r, KTH:KTH + 1], in1=sig2[:, r, :],
                        op0=ALU.is_ge, op1=ALU.mult)
                ins.then_inc(kept_ready, 1)

            def add_adjacency(t):
                dve.wait_ge(mixed_ready, t + 1)
                n = step(nc.vector.tensor_tensor(xn[:, :, :], mix_ps[:, :, :], kept2[:, :, :], ALU.add))
                dve.wait_ge(ln_mixed, t + 1)
                dve.wait_ge(vector_step, n)
                n = step(nc.vector.scalar_tensor_tensor(out=tiles(stream, t), in0=xn[:, :, :], scalar=quarter[:, 0:1],
                                                        in1=tiles(stream, t), op0=ALU.mult, op1=ALU.add))
                dve.wait_ge(vector_step, n)
                for r in range(R):
                    n = step(nc.vector.bn_stats(stat2[:, r, :], stream[:, R * t + r, :]))
                dve.wait_ge(vector_step, n - 1)
                nc.vector.bn_aggr(mv2[:, 0, :], stat2[:, 0, :]).then_inc(stats2_ready, 1)
                dve.wait_ge(vector_step, n)
                nc.vector.bn_aggr(mv2[:, 1, :], stat2[:, 1, :]).then_inc(stats2_ready, 1)

            def norm2(t):
                dve.wait_ge(rstd2_ready, t + 1)
                for r in range(R):
                    ins = nc.vector.tensor_scalar(xn[:, r, :], stream[:, R * t + r, :], mv2[:, r, 0:1],
                                                  rstd2[:, r:r + 1], ALU.subtract, ALU.mult)
                ins.then_inc(xn_ready, 1)

            def transpose_lo(t):
                dve.wait_ge(xt_hi_ready, t + 1)
                nc.vector.tensor_tensor(xt_lo[:, t, :], xt_ps[:, :, :].rearrange("p k n -> p (k n)"),
                                        xt_hi[:, t, :].bitcast(F32), ALU.subtract).then_inc(xt_lo_ready, 1)

            def gate(t):
                for r in range(R):
                    for e in range(E):
                        if r or e:
                            dve.wait_ge(vector_step, n)
                        ins = nc.vector.tensor_tensor_reduce(gate_prod[:, :], xn[:, r, :], gate_sb[:, e, :], 1.0, 0.0,
                                                             ALU.mult, ALU.add, logits[:, r, e:e + 1])
                        if r == R - 1 and e == E - 1:
                            ins.then_inc(logits_ready, 1)
                        else:
                            n = step(ins)

            def hidden(b, c):
                dve.wait_ge(silu_ready, CH * b + c + 1)
                nc.vector.tensor_tensor(h[:, c % RING, :], gu_ps[c % RING][:, 1, :], silu[:, c % 2, :],
                                        ALU.mult).then_inc(h_ready, 1)

            def add_expert(b, e):
                dve.wait_ge(y_ready[e], b + 1)
                if e == 0:
                    dve.wait_ge(weight_ready, b + 1)
                else:
                    dve.wait_ge(y_free[0], b + 2)
                for r in range(R):
                    i = R * b + r
                    ins = nc.vector.scalar_tensor_tensor(out=stream[:, i, :], in0=y_ps[e][:, r, :],
                                                         scalar=weight[:, i, e:e + 1], in1=stream[:, i, :],
                                                         op0=ALU.mult, op1=ALU.add)
                    if e == E - 1:
                        ins.then_inc(out_ready, 1)
                if e < E - 1:
                    ins.then_inc(y_free[e], 1)
                else:
                    dve.wait_ge(out_ready, R * (b + 1))
                    dve.sem_inc(y_free[e], 1)

            for e in range(E):
                dve.sem_inc(y_free[e], 1)
            dve.wait_ge(k_ready, 1)
            nc.vector.tensor_copy(qk_sb[:, 0, 1, :], gu_ps[1][0:C, 0, :]).then_inc(first_k_copied, 1)
            dve.wait_ge(gamma_ready, 1)
            nc.vector.tensor_scalar(quarter[:, :], gamma_th[:, :], 0.125, 0.125, ALU.mult, ALU.add)
            step(nc.vector.tensor_scalar(keep[:, :], gamma_th[:, :], -0.5, 0.5, ALU.mult, ALU.add))
            dve.wait_ge(x_in, 16)
            stats1(0, R)
            moments1(0, R)
            found, removed = [0, 0], [0, 0]
            for n in range(ROUNDS):
                rank(n, sim, found, removed)
                if n == 1:
                    scale1(0, R)
            keep_top(0)
            dve.wait_ge(x_rest_in, 16)
            stats1(R, 5)
            add_adjacency(0)
            stats1(5, B * R)
            norm2(0)
            moments1(R, B * R)
            transpose_lo(0)
            dve.wait_ge(gate_in, 16)
            for c in range(LAG):
                hidden(0, c)
                if c == 0:
                    gate(0)
            scale1(R, B * R)
            restart()
            with dve.Fori(0, B - 1) as b:
                found, removed = [0, 0], [0, 0]
                n = 0
                dve.wait_ge(left_ready, b + 1)
                for c in range(LAG, CH):
                    hidden(b, c)
                    for _ in range(RANKED_AT.count(c)):
                        rank(n, left, found, removed)
                        n += 1
                    if c == KEEP_AT:
                        keep_top(b + 1)
                    if c == KEEP_AT + 1:
                        add_adjacency(b + 1)
                    if c == KEEP_AT + 2:
                        norm2(b + 1)
                    if c == KEEP_AT + 3:
                        transpose_lo(b + 1)
                for c in range(LAG):
                    hidden(b + 1, c)
                    if c == 0:
                        gate(b + 1)
                    if c == 1:
                        add_expert(b, 0)
                add_expert(b, 1)
                restart()
            for c in range(LAG, CH):
                hidden(B - 1, c)
                if c == KEEP_AT:
                    add_expert(B - 1, 0)
            add_expert(B - 1, 1)

        @block.gpsimd
        def _(pool):
            def split_piece(i, piece):
                c = 2 * i + piece
                if piece < 2:
                    pool.wait_ge(w_hi_ready, 2 * i + 1)
                    nc.gpsimd.tensor_tensor(gu_lo[:, c, :, :, :].rearrange("p j k f -> p (j k f)"),
                                            stage_gu[:, i % STAGE, piece, :],
                                            gu_hi[:, c, :, :, :].rearrange("p j k f -> p (j k f)").bitcast(F32),
                                            ALU.subtract)
                else:
                    pool.wait_ge(w_hi_ready, 2 * i + 2)
                    nc.gpsimd.tensor_tensor(d_lo[:, 2 * i:2 * i + 2, :], stage_d[:, i, :, :],
                                            d_hi[:, 2 * i:2 * i + 2, :].bitcast(F32), ALU.subtract).then_inc(w_lo_ready, 1)

            def split_h(b, c):
                pool.wait_ge(h_hi_ready, CH * b + c + 1)
                nc.gpsimd.tensor_tensor(h_lo[:, c % RING, :], h[:, c % RING, :], h_hi[:, c % RING, :].bitcast(F32),
                                        ALU.subtract).then_inc(h_lo_ready, 1)

            def rstd_of_x(first, end):
                pool.wait_ge(stats1_ready, 1 if first == 0 else 2)
                nc.gpsimd.tensor_scalar(ve1[:, first:end], mv1[:, first:end, 1], EPS, None, ALU.add).then_inc(pool_step, 1)
                pool.wait_ge(pool_step, 1)
                nc.gpsimd.tensor_tensor(rstd1[:, first:end], ve1[:, first:end], minus_half[:, first:end],
                                        ALU.pow).then_inc(rstd1_ready, 1)
                pool.sem_clear(pool_step)

            def rstd_of_x1(t):
                pool.wait_ge(stats2_ready, R * (t + 1))
                nc.gpsimd.tensor_tensor(ve2[:, :], mv2[:, :, 1], eps[:, :], ALU.add).then_inc(pool_step, 1)
                pool.wait_ge(pool_step, 1)
                nc.gpsimd.tensor_tensor(rstd2[:, :], ve2[:, :], minus_half[:, 0:R], ALU.pow).then_inc(rstd2_ready, 1)
                pool.sem_clear(pool_step)

            def gate_margin(t):
                pool.wait_ge(logits_ready, t + 1)
                nc.gpsimd.tensor_tensor(margin[:, :], logits[:, :, 0], logits[:, :, 1], ALU.subtract).then_inc(margin_ready, 1)

            def expert_weights(t):
                for e, (sign, wins) in enumerate(((0.5, ALU.is_ge), (-0.5, ALU.is_lt))):
                    nc.gpsimd.tensor_scalar(prob[:, e, :], tanh_m[:, :], sign, 0.5, ALU.mult, ALU.add).then_inc(pool_step, 1)
                    nc.gpsimd.tensor_scalar(chosen[:, e, :], tanh_m[:, :], 0.0, None, wins).then_inc(pool_step, 1)
                for e in range(E):
                    pool.wait_ge(pool_step, 2 * e + 2)
                    ins = nc.gpsimd.tensor_tensor(weight[:, bass.ds(R * t, R), e], prob[:, e, :], chosen[:, e, :], ALU.mult)
                ins.then_inc(weight_ready, 1)
                pool.sem_clear(pool_step)

            nc.gpsimd.memset(minus_half[:, :], -0.5)
            nc.gpsimd.memset(eps[:, :], EPS)
            nc.gpsimd.memset(ident[:, :], 0.0).then_inc(const_step, 1)
            pool.wait_ge(const_step, 1)
            nc.gpsimd.affine_select(out=ident[:, :], in_=ident[:, :], compare_op=ALU.not_equal, fill=1.0, base=0,
                                    pattern=[[-1, P]], channel_multiplier=1).then_inc(const_ready, 1)
            rstd_of_x(0, R)
            for i in range(PAIRS_AHEAD - 1):
                for piece in range(3):
                    split_piece(i, piece)
            rstd_of_x1(0)
            for piece in range(3):
                split_piece(PAIRS_AHEAD - 1, piece)
            for c in range(CH):
                if c == 3:
                    pool.wait_ge(tanh_ready, 1)
                split_h(0, c)
                if c % 4 < 3 and PAIRS_AHEAD + c // 4 < PAIRS:
                    split_piece(PAIRS_AHEAD + c // 4, c % 4)
                if c == 1:
                    rstd_of_x(R, B * R)
                    gate_margin(0)
                if c == 3:
                    expert_weights(0)
                if c == KEEP_AT + 1:
                    rstd_of_x1(1)
            with pool.Fori(1, B - 1) as b:
                for c in range(CH):
                    if c == 3:
                        pool.wait_ge(tanh_ready, b + 1)
                    split_h(b, c)
                    if c == 1:
                        gate_margin(b)
                    if c == 3:
                        expert_weights(b)
                    if c == KEEP_AT + 1:
                        rstd_of_x1(b + 1)
            for c in range(CH):
                if c == 3:
                    pool.wait_ge(tanh_ready, B)
                split_h(B - 1, c)
                if c == 1:
                    gate_margin(B - 1)
                if c == 3:
                    expert_weights(B - 1)


def kernel(x, ctx_512, L0_xattn_Wq, L0_xattn_Wk, L0_xattn_gamma_raw, L0_ffn_gate_w, L0_ffn_w_gate, L0_ffn_w_up, L0_ffn_w_down):
    import numpy as np
    import concourse.bacc as bacc
    from concourse.bass_utils import run_bass_kernel_spmd

    B, N, D = x.shape
    E, F, _ = L0_ffn_w_gate.shape
    blocks = [np.asarray(w).reshape(E * F // P, P, D // P, P).transpose(3, 0, 2, 1) for w in (L0_ffn_w_gate, L0_ffn_w_up)]
    down = np.asarray(L0_ffn_w_down).reshape(E, D, F // P, P).transpose(3, 0, 2, 1)
    arrays = {
        "x": np.asarray(x).reshape(B * N, D),
        "ctx_t": np.asarray(ctx_512).reshape(B * N, -1).T,
        "wqk_t": np.stack([np.asarray(L0_xattn_Wq).T, np.asarray(L0_xattn_Wk).T], axis=1),
        "gamma_raw": np.asarray(L0_xattn_gamma_raw).reshape(1),
        "gate_w": np.asarray(L0_ffn_gate_w),
        "w_gate_up": np.stack(blocks, axis=2).reshape(P, E * F // P, 2 * D),
        "w_down": down.reshape(P, E * F // P, D),
    }
    arrays = {name: np.ascontiguousarray(a) for name, a in arrays.items()}
    nc = bacc.Bacc("TRN2", target_bir_lowering=False, num_devices=1)
    aps = [nc.dram_tensor(f"{name}_dram", a.shape, mybir.dt.from_np(a.dtype), kind="ExternalInput").ap()
           for name, a in arrays.items()]
    out = nc.dram_tensor("out_dram", (B * N, D), F32, kind="ExternalOutput").ap()
    xattn_ffn_kernel(nc, *aps, out)
    got = run_bass_kernel_spmd(nc, [{f"{name}_dram": a for name, a in arrays.items()}], core_ids=[0])
    return got.results[0]["out_dram"].reshape(B, N, D)
```

```python
from contextlib import ExitStack

import concourse.bass as bass
from concourse import mybir

ALU = mybir.AluOpType
ACT = mybir.ActivationFunctionType
F32 = mybir.dt.float32
F32R = mybir.dt.float32r

P = 128
EPS = 1e-5
LOWEST = -3.4028234e38
TOPK_RATIO = 0.3
HEADS = 4



def xattn_ffn_kernel(nc, x, ctx_t, wqk_t, gamma_raw, gate_w, w_gate_up, w_down, out):
    TOK, D = x.shape
    C = ctx_t.shape[0]
    KD = D // P
    CH = w_down.shape[1]
    E = gate_w.shape[0]
    CHE = CH // E
    N = D
    B = TOK // N
    R = N // P
    K = max(1, int(N * TOPK_RATIO))
    ROUNDS = -(-K // 8)
    KTH = (K - 1) % 8
    SIM_SCALE = 1.0 / ((C // HEADS) ** 0.5 * HEADS)
    RING = 4
    LAG = RING - 1
    KEEP_AT = ROUNDS
    XT_AT = KEEP_AT + 4
    RANKED_AT = [1] + list(range(1, KEEP_AT))
    PAIRS = CH // 2
    STAGE = PAIRS - 1
    LATE = PAIRS - 2
    PAIRS_AHEAD = 5
    LATER = [i for i in range(PAIRS_AHEAD, PAIRS) if i != LATE]
    PIECES_AT = [2, 3, 5, 7, 9, 10]
    RSTD_BEFORE = 3 * PAIRS_AHEAD - 4
    WARM = (13, 6, 5, 3, 10)
    assert B == 4 and R == 2 and KD == 2 and E == 2 and CH % RING == 0 and XT_AT < CH - 1
    assert PAIRS_AHEAD <= LATE and len(PIECES_AT) == 3 * len(LATER)

    x_tiles = x.rearrange("(t p) d -> p t d", p=P)
    out_tiles = out.rearrange("(t p) d -> p t d", p=P)

    with ExitStack() as stack:
        def sb(name, shape, dt=F32):
            return stack.enter_context(nc.sbuf_tensor(name, shape, dt))

        def pb(name, shape):
            return stack.enter_context(nc.psum_tensor(name, shape, F32))

        def sem(name):
            return stack.enter_context(nc.semaphore(name))

        stream = sb("stream", [P, B * R, D])
        ctx_sb = sb("ctx_sb", [C, TOK])
        wqk_sb = sb("wqk_sb", [C, 2, C])
        qk_sb = sb("qk_sb", [C, 2, 2, N])
        gamma_in = sb("gamma_in", [P, 1])
        gamma_th = sb("gamma_th", [P, 1])
        minus_keep = sb("minus_keep", [P, 1])
        quarter = sb("quarter", [P, 1])
        gate_sb = sb("gate_sb", [P, E, D])
        gate_prod = sb("gate_prod", [P, D])
        stage_gu = sb("stage_gu", [P, STAGE, 2, 2 * KD * P])
        stage_d = sb("stage_d", [P, PAIRS, 2, D])
        gu_hi = sb("gu_hi", [P, CH, 2, KD, P], F32R)
        gu_lo = sb("gu_lo", [P, CH, 2, KD, P], F32R)
        d_hi = sb("d_hi", [P, CH, D], F32R)
        d_lo = sb("d_lo", [P, CH, D], F32R)
        sim = sb("sim", [P, B * R, N])
        left = sb("left", [P, R, N])
        top8 = sb("top8", [P, 2, R, 8])
        sig2 = sb("sig2", [P, R, N])
        kept2 = sb("kept2", [P, R, N])
        xn = sb("xn", [P, R, D])
        stat1 = sb("stat1", [P, B * R, 6])
        mv1 = sb("mv1", [P, B * R, 2])
        ve1 = sb("ve1", [P, B * R])
        rstd1 = sb("rstd1", [P, B * R])
        a1 = sb("a1", [P, B * R])
        s1 = sb("s1", [P, B * R])
        b1 = sb("b1", [P, B * R])
        stat2 = sb("stat2", [P, R, 6])
        mv2 = sb("mv2", [P, R, 2])
        ve2 = sb("ve2", [P, R])
        rstd2 = sb("rstd2", [P, R])
        minus_half = sb("minus_half", [P, B * R])
        eps = sb("eps", [P, 1])
        ident = sb("ident", [P, P])
        zeros = sb("zeros", [P, N], mybir.dt.bfloat16)
        xt_hi = sb("xt_hi", [P, B, KD * N], F32R)
        xt_lo = sb("xt_lo", [P, B, KD * N], F32R)
        logits = sb("logits", [P, R, E])
        margin = sb("margin", [P, R])
        tanh_m = sb("tanh_m", [P, R])
        prob = sb("prob", [P, E, R])
        chosen = sb("chosen", [P, E, R])
        weight = sb("weight", [P, B * R, E])
        silu = sb("silu", [P, 2, N])
        h = sb("h", [P, RING, N])
        h_hi = sb("h_hi", [P, RING, N], F32R)
        h_lo = sb("h_lo", [P, RING, N], F32R)

        gu_ps = [pb(f"gu_ps{i}", [P, 2, N]) for i in range(RING)]
        y_ps = [pb(f"y_ps{e}", [P, R, D]) for e in range(E)]
        mix_ps = pb("mix_ps", [P, R, N])
        xt_ps = pb("xt_ps", [P, KD, N])

        ctx_in, wqk_in, x_in, gate_in = sem("ctx_in"), sem("wqk_in"), sem("x_in"), sem("gate_in")
        gamma_landed = sem("gamma_landed")
        ctx_rest_in = sem("ctx_rest_in")
        x_rest_in = sem("x_rest_in")
        w_in = [sem(f"w_in{i}") for i in range(PAIRS)]
        q_ready, k_ready, sim_ready, mixed_ready = sem("q_ready"), sem("k_ready"), sem("sim_ready"), sem("mixed_ready")
        first_q_ready = sem("first_q_ready")
        xt_ready, gu_ready = sem("xt_ready"), sem("gu_ready")
        y_ready = [sem(f"y_ready{e}") for e in range(E)]
        gamma_ready, q_copied, k_copied, sim_copied = sem("gamma_ready"), sem("q_copied"), sem("k_copied"), sem("sim_copied")
        left_ready, sig_raw, sig_ready, ln_mixed = sem("left_ready"), sem("sig_raw"), sem("sig_ready"), sem("ln_mixed")
        w_hi_ready, xt_hi_ready, tanh_ready = sem("w_hi_ready"), sem("xt_hi_ready"), sem("tanh_ready")
        silu_ready, h_hi_ready = sem("silu_ready"), sem("h_hi_ready")
        zeros_ready, first_removed = sem("zeros_ready"), sem("first_removed")
        first_q_copied, late_lo_ready = sem("first_q_copied"), sem("late_lo_ready")
        vector_step, stats1_ready = sem("vector_step"), sem("stats1_ready")
        ranked, kept_ready, stats2_ready = sem("ranked"), sem("kept_ready"), sem("stats2_ready")
        xn_ready, xt_lo_ready, logits_ready = sem("xn_ready"), sem("xt_lo_ready"), sem("logits_ready")
        h_ready, y_free = sem("h_ready"), [sem(f"y_free{e}") for e in range(E)]
        out_ready = sem("out_ready")
        const_step, const_ready, w_lo_ready = sem("const_step"), sem("const_ready"), sem("w_lo_ready")
        pool_step, ln1_ready, rstd2_ready = sem("pool_step"), sem("ln1_ready"), sem("rstd2_ready")
        h_lo_ready, margin_ready, weight_ready = sem("h_lo_ready"), sem("margin_ready"), sem("weight_ready")
        out_stored, last_stored = sem("out_stored"), sem("last_stored")

        def tiles(ap, t):
            return ap[:, bass.ds(R * t, R), :]

        block = stack.enter_context(nc.Block())

        @block.sync
        def _(sp):
            sp.dma_start(ctx_sb[:, 0:N], ctx_t[:, 0:N]).then_inc(ctx_in, 16)
            sp.dma_start(stream[:, 0:R, :], x_tiles[:, 0:R, :]).then_inc(x_in, 16)
            for i in range(PAIRS):
                if i == 1:
                    sp.dma_start(ctx_sb[:, N:], ctx_t[:, N:]).then_inc(ctx_rest_in, 16)
                if i == 2:
                    sp.dma_start(stream[:, R:, :], x_tiles[:, R:, :]).then_inc(x_rest_in, 16)
                if i >= STAGE:
                    sp.wait_ge(w_lo_ready, i - STAGE + 1)
                sp.dma_start(stage_gu[:, i % STAGE, :, :],
                             w_gate_up[:, 2 * i:2 * i + 2, :]).then_inc(w_in[i], 16)
                sp.dma_start(stage_d[:, i, :, :], w_down[:, 2 * i:2 * i + 2, :]).then_inc(w_in[i], 16)
            with sp.Fori(0, B * R - 1) as i:
                sp.wait_ge(out_ready, i + 1)
                sp.dma_start(out_tiles[:, i, :], stream[:, i, :]).then_inc(out_stored, 16)
            sp.wait_ge(out_stored, 16 * (B * R - 1))
            sp.wait_ge(last_stored, 16)

        @block.tensor
        def _(pe):
            def keep_warm(count):
                for _ in range(count):
                    pe.matmul(y_ps[0][:, 0, :], zeros[:, 0:P], zeros[:, :], start=True, stop=True)

            def project(t):
                if t == 0:
                    pe.wait_ge(ctx_in, 16)
                    pe.wait_ge(wqk_in, 16)
                if t == 1:
                    pe.wait_ge(ctx_rest_in, 16)
                q, k = wqk_sb[:, 0, :], wqk_sb[:, 1, :]
                pe.matmul(gu_ps[1][0:C, 0, :], k, ctx_sb[:, N * t:N * (t + 1)], start=True, stop=True).then_inc(k_ready, 1)
                if t == 0:
                    pe.matmul(gu_ps[0][0:C, 0, 0:P], q, ctx_sb[:, 0:P], start=True, stop=True).then_inc(first_q_ready, 1)
                    pe.matmul(xt_ps[0:C, 0, 0:P], q, ctx_sb[:, P:N], start=True, stop=True).then_inc(q_ready, 1)
                else:
                    pe.matmul(gu_ps[0][0:C, 0, :], q, ctx_sb[:, N * t:N * (t + 1)], start=True, stop=True).then_inc(q_ready, 1)

            def similarities(t):
                pe.wait_ge(k_copied, t + 1)
                if t:
                    pe.wait_ge(q_copied, t + 1)
                    pe.wait_ge(sim_copied, R * t)
                else:
                    pe.wait_ge(first_q_copied, 1)
                for r in range(R):
                    if r == 1 and t == 0:
                        pe.wait_ge(q_copied, 1)
                    pe.matmul(gu_ps[2 + r][:, 0, :], qk_sb[:, t % 2, 0, P * r:P * (r + 1)], qk_sb[:, t % 2, 1, :],
                              start=True, stop=True).then_inc(sim_ready, 1)

            def transpose_kept(t):
                pe.wait_ge(kept_ready, t + 1)
                for r in range(R):
                    for s in range(R):
                        mm = pe.transpose(mix_ps[:, r, P * s:P * (s + 1)], kept2[:, s, P * r:P * (r + 1)], ident[:, :])
                mm.then_inc(mixed_ready, 1)

            def transpose_xn(t):
                for r in range(R):
                    pe.wait_ge(xn_ready, R * t + r + 1)
                    for k in range(KD):
                        mm = pe.transpose(xt_ps[:, k, P * r:P * (r + 1)], xn[:, r, P * k:P * (k + 1)], ident[:, :])
                mm.then_inc(xt_ready, 1)

            def up(b, c, first):
                if c // 2 == LATE:
                    pe.wait_ge(late_lo_ready, 1)
                else:
                    pe.wait_ge(w_lo_ready, c // 2 + (c // 2 < LATE))
                if c == 0:
                    pe.wait_ge(xt_hi_ready, b + 1)
                if c in (2, 3) and first:
                    pe.wait_ge(sim_copied, R * (B - 1) + c - 1)
                for j in range(2):
                    n = 0
                    for w, xt in ((gu_hi, xt_hi), (gu_lo, xt_hi), (gu_hi, xt_lo)):
                        if c == 0 and j == 0 and xt is xt_lo:
                            pe.wait_ge(xt_lo_ready, b + 1)
                        for k in range(KD):
                            mm = pe.matmul(gu_ps[c % RING][:, j, :], w[:, c, j, k, :],
                                           xt[:, b, k * N:(k + 1) * N],
                                           start=(n == 0), stop=(n == 3 * KD - 1))
                            n += 1
                mm.then_inc(gu_ready, 1)

            def down(b, c, first):
                e = c // CHE
                if first and c == 2 * LATE:
                    pe.wait_ge(late_lo_ready, 2)
                if c % CHE == 0:
                    pe.wait_ge(y_free[e], b + 1)
                pe.wait_ge(h_hi_ready, CH * b + c + 1)
                for i, (a, w) in enumerate(((h_hi, d_hi), (h_hi, d_lo), (h_lo, d_hi))):
                    if a is h_lo:
                        pe.wait_ge(h_lo_ready, CH * b + c + 1)
                    for r in range(R):
                        mm = pe.matmul(y_ps[e][:, r, :], a[:, c % RING, P * r:P * (r + 1)], w[:, c, :],
                                       start=(c % CHE == 0 and r == 0 and i == 0),
                                       stop=(c % CHE == CHE - 1 and i == 2), skip_group_check=True)
                if c % CHE == CHE - 1:
                    mm.then_inc(y_ready[e], 1)

            def batch(b, first=False, last=False):
                for c in range(CH):
                    up(b, c, first)
                    if c == XT_AT and not last:
                        transpose_xn(b + 1)
                    if c >= LAG:
                        down(b, c - LAG, first)
                    elif not first:
                        down(b - 1, CH - LAG + c, first)
                    if c == KEEP_AT + 1 and not last:
                        transpose_kept(b + 1)
                if last:
                    for c in range(CH - LAG, CH):
                        down(b, c, first)

            pe.wait_ge(zeros_ready, 1)
            keep_warm(WARM[0])
            project(0)
            similarities(0)
            project(1)
            similarities(1)
            project(2)
            keep_warm(WARM[1])
            similarities(2)
            pe.wait_ge(const_ready, 1)
            keep_warm(WARM[2])
            transpose_kept(0)
            keep_warm(WARM[3])
            project(3)
            keep_warm(WARM[4])
            transpose_xn(0)
            similarities(3)
            batch(0, first=True)
            with pe.Fori(1, B - 1) as b:
                batch(b)
            batch(B - 1, last=True)

        @block.scalar
        def _(act):
            act.dma_start(wqk_sb[:, :, :], wqk_t).then_inc(wqk_in, 16)
            act.dma_start(gamma_in[:, :], gamma_raw.partition_broadcast(P)).then_inc(gamma_landed, 16)
            act.preload_act_table(ACT.Silu)
            act.wait_ge(gamma_landed, 16)
            nc.scalar.activation(gamma_th[:, :], gamma_in[:, :], ACT.Tanh, scale=0.5).then_inc(gamma_ready, 1)

            def copy_projections(t):
                act.wait_ge(k_ready, t + 1)
                nc.scalar.copy(qk_sb[:, t % 2, 1, :], gu_ps[1][0:C, 0, :]).then_inc(k_copied, 1)
                act.wait_ge(q_ready, t + 1)
                if t == 0:
                    nc.scalar.copy(qk_sb[:, 0, 0, P:N], xt_ps[0:C, 0, 0:P]).then_inc(q_copied, 1)
                else:
                    nc.scalar.copy(qk_sb[:, t % 2, 0, :], gu_ps[0][0:C, 0, :]).then_inc(q_copied, 1)

            def copy_sim(t):
                for r in range(R):
                    act.wait_ge(sim_ready, R * t + r + 1)
                    if t == 0:
                        act.wait_ge(first_removed, r + 1)
                    nc.scalar.copy(sim[:, R * t + r, :], gu_ps[2 + r][:, 0, :]).then_inc(sim_copied, 1)

            def sigmoid2(t):
                nc.scalar.activation(sig2[:, :, :], tiles(sim, t), ACT.Tanh, scale=0.5 * SIM_SCALE).then_inc(sig_raw, 1)
                act.wait_ge(sig_raw, t + 1)
                nc.scalar.add(sig2[:, :, :], sig2[:, :, :], 1.0).then_inc(sig_ready, 1)

            def mix_ln1(t, r):
                i = R * t + r
                ins = nc.scalar.activation(stream[:, i, :], stream[:, i, :], ACT.Identity,
                                           scale=s1[:, bass.ds(i, 1)], bias=b1[:, bass.ds(i, 1)])
                if r == R - 1:
                    ins.then_inc(ln_mixed, 1)

            def split_gate_up(i):
                act.wait_ge(w_in[i], 32)
                nc.scalar.copy(gu_hi[:, 2 * i:2 * i + 2, :, :, :].rearrange("p c j k f -> p c (j k f)"),
                               stage_gu[:, i % STAGE, :, :]).then_inc(w_hi_ready, 1)

            def split_down(i):
                nc.scalar.copy(d_hi[:, 2 * i:2 * i + 2, :], stage_d[:, i, :, :]).then_inc(w_hi_ready, 1)

            def split_weights(i):
                split_gate_up(i)
                split_down(i)

            def transpose_hi(t):
                nc.scalar.copy(xt_hi[:, t, :], xt_ps[:, :, :].rearrange("p k n -> p (k n)")).then_inc(xt_hi_ready, 1)

            def gate_tanh(t):
                act.wait_ge(margin_ready, t + 1)
                nc.scalar.activation(tanh_m[:, :], margin[:, :], ACT.Tanh, scale=0.5).then_inc(tanh_ready, 1)

            def silu_of(b, c):
                act.wait_ge(gu_ready, CH * b + c + 1)
                nc.scalar.activation(silu[:, c % 2, :], gu_ps[c % RING][:, 0, :], ACT.Silu).then_inc(silu_ready, 1)

            def split_h(b, c):
                act.wait_ge(h_ready, CH * b + c + 1)
                nc.scalar.copy(h_hi[:, c % RING, :], h[:, c % RING, :]).then_inc(h_hi_ready, 1)

            copy_projections(0)
            split_weights(0)
            copy_sim(0)
            act.wait_ge(sim_copied, R)
            sigmoid2(0)
            split_weights(1)
            act.wait_ge(ln1_ready, 2)
            mix_ln1(0, 0)
            mix_ln1(0, 1)
            act.dma_start(gate_sb[:, :, :], gate_w.partition_broadcast(P)).then_inc(gate_in, 16)
            copy_projections(1)
            split_weights(2)
            copy_sim(1)
            copy_projections(2)
            split_weights(3)
            copy_sim(2)
            split_weights(4)
            split_weights(5)
            copy_projections(3)
            split_weights(LATE)
            act.wait_ge(xt_ready, 1)
            transpose_hi(0)
            copy_sim(3)

            def batch(b, first=False, last=False):
                for c in range(CH):
                    silu_of(b, c)
                    if c == 0 and not last:
                        act.wait_ge(ranked, b + 1)
                    if c == 1 and not last:
                        act.wait_ge(kept_ready, b + 1)
                    if c == XT_AT and not last:
                        act.wait_ge(xt_ready, b + 2)
                    if c:
                        split_h(b, c - 1)
                    elif not first:
                        split_h(b - 1, CH - 1)
                    if c == 0 and not last:
                        nc.scalar.copy(left[:, :, :], tiles(sim, b + 1)).then_inc(left_ready, 1)
                    if c == 1 and not last:
                        sigmoid2(b + 1)
                    if c == 2 and first:
                        split_gate_up(PAIRS - 1)
                    if c == 3 and first:
                        split_down(PAIRS - 1)
                    if c == 3:
                        gate_tanh(b)
                    if c in (4, 5) and not last:
                        if c == 4:
                            act.wait_ge(ln1_ready, 4)
                        mix_ln1(b + 1, c - 4)
                    if c == XT_AT and not last:
                        transpose_hi(b + 1)
                if last:
                    split_h(b, CH - 1)

            batch(0, first=True)
            with act.Fori(1, B - 1) as b:
                batch(b)
            batch(B - 1, last=True)
            act.wait_ge(out_ready, B * R)
            act.dma_start(out_tiles[:, B * R - 1, :], stream[:, B * R - 1, :]).then_inc(last_stored, 16)

        @block.vector
        def _(dve):
            steps = [0]

            def step(ins):
                ins.then_inc(vector_step, 1)
                steps[0] += 1
                return steps[0]

            def restart():
                dve.wait_ge(vector_step, steps[0])
                dve.sem_clear(vector_step)
                steps[0] = 0

            def stats1(first, end):
                for i in range(first, end):
                    step(nc.vector.bn_stats(stat1[:, i, :], stream[:, i, :]))

            def moments1(first, end):
                dve.wait_ge(vector_step, steps[0])
                for i in range(first, end):
                    ins = nc.vector.bn_aggr(mv1[:, i, :], stat1[:, i, :])
                ins.then_inc(stats1_ready, 1)

            def rank(n, found, removed):
                for r in range(R):
                    if n:
                        dve.wait_ge(vector_step, removed[r])
                    ins = nc.vector.max(top8[:, n % 2, r, :], left[:, r, :])
                    if n == ROUNDS - 1 and r == R - 1:
                        ins.then_inc(ranked, 1)
                    else:
                        found[r] = step(ins)
                if n == ROUNDS - 1:
                    return
                for r in range(R):
                    dve.wait_ge(vector_step, found[r])
                    removed[r] = step(nc.vector.match_replace(left[:, r, :], top8[:, n % 2, r, :], left[:, r, :], LOWEST))

            def rank_first(removed):
                for r in range(R):
                    dve.wait_ge(sim_ready, r + 1)
                    n = step(nc.vector.max(top8[:, 0, r, :], gu_ps[2 + r][:, 0, :]))
                    dve.wait_ge(vector_step, n)
                    nc.vector.match_replace(left[:, r, :], top8[:, 0, r, :], gu_ps[2 + r][:, 0, :],
                                            LOWEST).then_inc(first_removed, 1)

            late, after_late = 2 * LATE, 2 * LATE + 2

            def split_late_gate_up():
                dve.wait_ge(w_hi_ready, 2 * LATE + 1)
                nc.vector.tensor_tensor(gu_lo[:, late:after_late, :, :, :].rearrange("p c j k f -> p c (j k f)"),
                                        stage_gu[:, LATE % STAGE, :, :],
                                        gu_hi[:, late:after_late, :, :, :].rearrange("p c j k f -> p c (j k f)").bitcast(F32),
                                        ALU.subtract).then_inc(late_lo_ready, 1)

            def split_late_down():
                dve.wait_ge(w_hi_ready, 2 * LATE + 2)
                nc.vector.tensor_tensor(d_lo[:, late:after_late, :], stage_d[:, LATE, :, :],
                                        d_hi[:, late:after_late, :].bitcast(F32), ALU.subtract).then_inc(late_lo_ready, 1)

            def keep_top(t):
                dve.wait_ge(ranked, t + 1)
                dve.wait_ge(sig_ready, t + 1)
                for r in range(R):
                    ins = nc.vector.scalar_tensor_tensor(
                        out=kept2[:, r, :], in0=sim[:, R * t + r, :],
                        scalar=top8[:, (ROUNDS - 1) % 2, r, KTH:KTH + 1], in1=sig2[:, r, :],
                        op0=ALU.is_ge, op1=ALU.mult)
                ins.then_inc(kept_ready, 1)
                dve.wait_ge(ln_mixed, t + 1)
                dve.wait_ge(kept_ready, t + 1)
                return step(nc.vector.scalar_tensor_tensor(out=tiles(stream, t), in0=kept2[:, :, :], scalar=quarter[:, 0:1],
                                                           in1=tiles(stream, t), op0=ALU.mult, op1=ALU.add))

            def add_transposed(t, kept_added):
                dve.wait_ge(mixed_ready, t + 1)
                dve.wait_ge(vector_step, kept_added)
                n = step(nc.vector.scalar_tensor_tensor(out=tiles(stream, t), in0=mix_ps[:, :, :], scalar=quarter[:, 0:1],
                                                        in1=tiles(stream, t), op0=ALU.mult, op1=ALU.add))
                dve.wait_ge(vector_step, n)
                for r in range(R):
                    n = step(nc.vector.bn_stats(stat2[:, r, :], stream[:, R * t + r, :]))
                    dve.wait_ge(vector_step, n)
                    nc.vector.bn_aggr(mv2[:, r, :], stat2[:, r, :]).then_inc(stats2_ready, 1)

            def norm2(t):
                for r in range(R):
                    dve.wait_ge(rstd2_ready, R * t + r + 1)
                    nc.vector.tensor_scalar(xn[:, r, :], stream[:, R * t + r, :], mv2[:, r, 0:1],
                                            rstd2[:, r:r + 1], ALU.subtract, ALU.mult).then_inc(xn_ready, 1)

            def transpose_lo(t):
                dve.wait_ge(xt_hi_ready, t + 1)
                nc.vector.tensor_tensor(xt_lo[:, t, :], xt_ps[:, :, :].rearrange("p k n -> p (k n)"),
                                        xt_hi[:, t, :].bitcast(F32), ALU.subtract).then_inc(xt_lo_ready, 1)

            def gate(t):
                for r in range(R):
                    for e in range(E):
                        if r or e:
                            dve.wait_ge(vector_step, n)
                        ins = nc.vector.tensor_tensor_reduce(gate_prod[:, :], xn[:, r, :], gate_sb[:, e, :], 1.0, 0.0,
                                                             ALU.mult, ALU.add, logits[:, r, e:e + 1])
                        if r == R - 1 and e == E - 1:
                            ins.then_inc(logits_ready, 1)
                        else:
                            n = step(ins)

            def hidden(b, c):
                dve.wait_ge(silu_ready, CH * b + c + 1)
                nc.vector.tensor_tensor(h[:, c % RING, :], gu_ps[c % RING][:, 1, :], silu[:, c % 2, :],
                                        ALU.mult).then_inc(h_ready, 1)

            def add_expert(b, e):
                dve.wait_ge(y_ready[e], b + 1)
                if e == 0:
                    dve.wait_ge(weight_ready, b + 1)
                else:
                    dve.wait_ge(y_free[0], b + 2)
                for r in range(R):
                    i = R * b + r
                    ins = nc.vector.scalar_tensor_tensor(out=stream[:, i, :], in0=y_ps[e][:, r, :],
                                                         scalar=weight[:, i, e:e + 1], in1=stream[:, i, :],
                                                         op0=ALU.mult, op1=ALU.add)
                    if e == E - 1:
                        ins.then_inc(out_ready, 1)
                if e < E - 1:
                    ins.then_inc(y_free[e], 1)
                else:
                    dve.wait_ge(out_ready, R * (b + 1))
                    dve.sem_inc(y_free[e], 1)

            nc.vector.memset(zeros[:, :], 0.0).then_inc(zeros_ready, 1)
            for e in range(E):
                dve.sem_inc(y_free[e], 1)
            dve.wait_ge(first_q_ready, 1)
            nc.vector.tensor_copy(qk_sb[:, 0, 0, 0:P], gu_ps[0][0:C, 0, 0:P]).then_inc(first_q_copied, 1)
            dve.wait_ge(gamma_ready, 1)
            nc.vector.tensor_scalar(quarter[:, :], gamma_th[:, :], 0.125, 0.125, ALU.mult, ALU.add)
            step(nc.vector.tensor_scalar(minus_keep[:, :], gamma_th[:, :], 0.5, -0.5, ALU.mult, ALU.add))
            dve.wait_ge(x_in, 16)
            stats1(0, R)
            moments1(0, R)
            found, removed = [0, 0], [0, 0]
            rank_first(removed)
            dve.wait_ge(first_removed, R)
            for n in range(1, ROUNDS):
                rank(n, found, removed)
            kept_added = keep_top(0)
            dve.wait_ge(x_rest_in, 16)
            stats1(R, R + 1)
            add_transposed(0, kept_added)
            stats1(R + 1, R + 2)
            norm2(0)
            stats1(R + 2, B * R - 1)
            transpose_lo(0)
            split_late_gate_up()
            stats1(B * R - 1, B * R)
            moments1(R, B * R)
            dve.wait_ge(gate_in, 16)
            restart()

            def batch(b, first=False, last=False):
                found, removed = [0, 0], [0, 0]
                n = 0
                if not last:
                    dve.wait_ge(left_ready, b + 1)
                for c in range(CH):
                    hidden(b, c)
                    if c == 0:
                        gate(b)
                    if c == LAG and not first:
                        add_expert(b - 1, E - 1)
                    for _ in range(0 if last else RANKED_AT.count(c)):
                        rank(n, found, removed)
                        n += 1
                    if c == KEEP_AT and not last:
                        kept_added = keep_top(b + 1)
                    if c == KEEP_AT + 1:
                        add_expert(b, 0)
                        if not last:
                            add_transposed(b + 1, kept_added)
                    if c == KEEP_AT + 2 and not last:
                        norm2(b + 1)
                    if c == KEEP_AT + 2 and first:
                        split_late_down()
                    if c == XT_AT and not last:
                        transpose_lo(b + 1)
                if last:
                    add_expert(b, E - 1)
                restart()

            batch(0, first=True)
            with dve.Fori(1, B - 1) as b:
                batch(b)
            batch(B - 1, last=True)

        @block.gpsimd
        def _(pool):
            def split_piece(i, piece):
                c = 2 * i + piece
                if piece < 2:
                    pool.wait_ge(w_hi_ready, 2 * i + 1)
                    nc.gpsimd.tensor_tensor(gu_lo[:, c, :, :, :].rearrange("p j k f -> p (j k f)"),
                                            stage_gu[:, i % STAGE, piece, :],
                                            gu_hi[:, c, :, :, :].rearrange("p j k f -> p (j k f)").bitcast(F32),
                                            ALU.subtract)
                else:
                    pool.wait_ge(w_hi_ready, 2 * i + 2)
                    nc.gpsimd.tensor_tensor(d_lo[:, 2 * i:2 * i + 2, :], stage_d[:, i, :, :],
                                            d_hi[:, 2 * i:2 * i + 2, :].bitcast(F32), ALU.subtract).then_inc(w_lo_ready, 1)

            def split_h(b, c):
                pool.wait_ge(h_hi_ready, CH * b + c + 1)
                nc.gpsimd.tensor_tensor(h_lo[:, c % RING, :], h[:, c % RING, :], h_hi[:, c % RING, :].bitcast(F32),
                                        ALU.subtract).then_inc(h_lo_ready, 1)

            def scale_of_x(first, end):
                pool.wait_ge(stats1_ready, 1 if first == 0 else 2)
                nc.gpsimd.tensor_scalar(ve1[:, first:end], mv1[:, first:end, 1], EPS, None, ALU.add).then_inc(pool_step, 1)
                pool.wait_ge(pool_step, 1)
                nc.gpsimd.tensor_tensor(rstd1[:, first:end], ve1[:, first:end], minus_half[:, first:end],
                                        ALU.pow).then_inc(pool_step, 1)
                pool.wait_ge(pool_step, 2)
                nc.gpsimd.tensor_scalar(a1[:, first:end], rstd1[:, first:end], minus_keep[:, 0:1], None,
                                        ALU.mult).then_inc(pool_step, 1)
                pool.wait_ge(pool_step, 3)
                nc.gpsimd.tensor_scalar(s1[:, first:end], a1[:, first:end], -1.0, 1.0, ALU.mult,
                                        ALU.add).then_inc(ln1_ready, 1)
                nc.gpsimd.tensor_tensor(b1[:, first:end], mv1[:, first:end, 0], a1[:, first:end],
                                        ALU.mult).then_inc(ln1_ready, 1)
                pool.sem_clear(pool_step)

            def rstd_of_x1(t):
                for r in range(R):
                    pool.wait_ge(stats2_ready, R * t + r + 1)
                    nc.gpsimd.tensor_tensor(ve2[:, r:r + 1], mv2[:, r, 1:2], eps[:, :], ALU.add).then_inc(pool_step, 1)
                    pool.wait_ge(pool_step, r + 1)
                    nc.gpsimd.tensor_tensor(rstd2[:, r:r + 1], ve2[:, r:r + 1], minus_half[:, 0:1],
                                            ALU.pow).then_inc(rstd2_ready, 1)
                pool.sem_clear(pool_step)

            def gate_margin(t):
                pool.wait_ge(logits_ready, t + 1)
                nc.gpsimd.tensor_tensor(margin[:, :], logits[:, :, 0], logits[:, :, 1], ALU.subtract).then_inc(margin_ready, 1)

            def expert_weights(t):
                for e, (sign, wins) in enumerate(((0.5, ALU.is_ge), (-0.5, ALU.is_lt))):
                    nc.gpsimd.tensor_scalar(prob[:, e, :], tanh_m[:, :], sign, 0.5, ALU.mult, ALU.add).then_inc(pool_step, 1)
                    nc.gpsimd.tensor_scalar(chosen[:, e, :], tanh_m[:, :], 0.0, None, wins).then_inc(pool_step, 1)
                for e in range(E):
                    pool.wait_ge(pool_step, 2 * e + 2)
                    ins = nc.gpsimd.tensor_tensor(weight[:, bass.ds(R * t, R), e], prob[:, e, :], chosen[:, e, :], ALU.mult)
                ins.then_inc(weight_ready, 1)
                pool.sem_clear(pool_step)

            nc.gpsimd.memset(minus_half[:, :], -0.5)
            nc.gpsimd.memset(eps[:, :], EPS)
            nc.gpsimd.memset(ident[:, :], 0.0).then_inc(const_step, 1)
            pool.wait_ge(const_step, 1)
            nc.gpsimd.affine_select(out=ident[:, :], in_=ident[:, :], compare_op=ALU.not_equal, fill=1.0, base=0,
                                    pattern=[[-1, P]], channel_multiplier=1).then_inc(const_ready, 1)
            split_piece(0, 0)
            scale_of_x(0, R)
            for piece in range(1, 3 * PAIRS_AHEAD):
                if piece == RSTD_BEFORE:
                    rstd_of_x1(0)
                split_piece(piece // 3, piece % 3)

            def batch(b, first=False, last=False):
                for c in range(CH):
                    if c == 4:
                        pool.wait_ge(tanh_ready, b + 1)
                    split_h(b, c)
                    if c == 0 and first:
                        scale_of_x(R, B * R)
                    if c == 1:
                        gate_margin(b)
                    if c == 4:
                        expert_weights(b)
                    if c == KEEP_AT + 1 and not last:
                        rstd_of_x1(b + 1)
                    if first and c in PIECES_AT:
                        piece = PIECES_AT.index(c)
                        split_piece(LATER[piece // 3], piece % 3)

            batch(0, first=True)
            with pool.Fori(1, B - 1) as b:
                batch(b)
            batch(B - 1, last=True)


def kernel(x, ctx_512, L0_xattn_Wq, L0_xattn_Wk, L0_xattn_gamma_raw, L0_ffn_gate_w, L0_ffn_w_gate, L0_ffn_w_up, L0_ffn_w_down):
    import numpy as np
    import concourse.bacc as bacc
    from concourse.bass_utils import run_bass_kernel_spmd

    B, N, D = x.shape
    E, F, _ = L0_ffn_w_gate.shape
    blocks = [np.asarray(w).reshape(E * F // P, P, D // P, P).transpose(3, 0, 2, 1) for w in (L0_ffn_w_gate, L0_ffn_w_up)]
    down = np.asarray(L0_ffn_w_down).reshape(E, D, F // P, P).transpose(3, 0, 2, 1)
    arrays = {
        "x": np.asarray(x).reshape(B * N, D),
        "ctx_t": np.asarray(ctx_512).reshape(B * N, -1).T,
        "wqk_t": np.stack([np.asarray(L0_xattn_Wq).T, np.asarray(L0_xattn_Wk).T], axis=1),
        "gamma_raw": np.asarray(L0_xattn_gamma_raw).reshape(1),
        "gate_w": np.asarray(L0_ffn_gate_w),
        "w_gate_up": np.stack(blocks, axis=2).reshape(P, E * F // P, 2 * D),
        "w_down": down.reshape(P, E * F // P, D),
    }
    arrays = {name: np.ascontiguousarray(a) for name, a in arrays.items()}
    nc = bacc.Bacc("TRN2", target_bir_lowering=False, num_devices=1)
    aps = [nc.dram_tensor(f"{name}_dram", a.shape, mybir.dt.from_np(a.dtype), kind="ExternalInput").ap()
           for name, a in arrays.items()]
    out = nc.dram_tensor("out_dram", (B * N, D), F32, kind="ExternalOutput").ap()
    xattn_ffn_kernel(nc, *aps, out)
    got = run_bass_kernel_spmd(nc, [{f"{name}_dram": a for name, a in arrays.items()}], core_ids=[0])
    return got.results[0]["out_dram"].reshape(B, N, D)
```
